# Optimizing a Trainium2 kernel written in Bass

```python
import numpy as np
import jax
import jax.numpy as jnp

def _softmax(x, axis=-1):
    return jax.nn.softmax(x, axis=axis)

def _gelu(x):
    return jax.nn.gelu(x, approximate=True)

def _silu(x):
    return jax.nn.silu(x)

def _sigmoid(x):
    return jax.nn.sigmoid(x)

def _layernorm(x, axis=-1, eps=1e-05):
    m = jnp.mean(x, axis=axis, keepdims=True)
    v = jnp.var(x, axis=axis, keepdims=True)
    return (x - m) / jnp.sqrt(v + eps)

def _scatter_add(tgt, idx, src, axis=0):
    return tgt.at[idx].add(src)

def _segment_sum(src, seg, n):
    return jax.ops.segment_sum(src, seg, n)
kernel_name = 'mk_xattn_ffn_d1_seqx_r4_fa3e8d'

def setup_inputs(seed: int=0):
    np.random.seed(seed)
    _w = jnp.asarray

    def _rec_inputs():
        import jax
        import jax.numpy as jnp
        _rk = jax.random.key(seed)
        x = -0.0002928 + 1 * jax.random.normal(jax.random.fold_in(_rk, 1), (8, 256, 512), jnp.float32)
        _lenS = 256 - jax.random.randint(jax.random.fold_in(_rk, 7), (8,), 0, max(1, 256 // 4) + 1, jnp.int32)
        _lenS2 = 256 - jax.random.randint(jax.random.fold_in(_rk, 8), (8,), 0, max(1, 256 // 4) + 1, jnp.int32)
        fside_S2_0 = -0.00337071 + 1.01897 * jax.random.normal(jax.random.fold_in(_rk, 11), (256,), jnp.float32)
        _ctx_2048P = jax.random.normal(jax.random.fold_in(_rk, 12), (8, 16, 512), jnp.float32)
        _ctx_2048c = jax.random.dirichlet(jax.random.fold_in(_rk, 512), 0.3 * jnp.ones((16,), jnp.float32), (8, 256))
        _ctx_2048t = jnp.einsum('bsk,bkd->bsd', _ctx_2048c, _ctx_2048P)
        _ctx_2048t = _ctx_2048t * jax.lax.rsqrt(jnp.mean(jnp.square(_ctx_2048t)) + 1e-12) * 0.953939
        ctx_2048 = 0.000675642 + 1.00031 * (_ctx_2048t + 0.3 * jax.random.normal(jax.random.fold_in(_rk, 612), (8, 256, 512), jnp.float32))
        return (x, fside_S2_0, ctx_2048)
    x, fside_S2_0, ctx_2048 = _rec_inputs()

    def _L0_xattn_setup():
        import jax, jax.numpy as jnp
        import numpy as np
        key = jax.random.key(seed)
        ks = jax.random.split(key, 5)
        B, D, L, NH = (2, 256, 512, 8)
        H = D // NH
        return {'v': jax.random.normal(ks[0], (B, D, L), jnp.float32), 'k': jax.random.normal(ks[1], (H, L), jnp.float32) * 0.1, 'bias': jax.random.normal(ks[2], (D,), jnp.float32), 'x1': jax.random.normal(ks[3], (B, D, L), jnp.float32), 'x2': jax.random.normal(ks[4], (B, D, L), jnp.float32), 'num_heads': NH}
    _L0_xattn_all = _L0_xattn_setup()
    _L0_xattn_in = {k: v for k, v in _L0_xattn_all.items() if k in ('k',)}
    del _L0_xattn_all

    def _L0_ffn_setup():
        import jax, jax.numpy as jnp
        import numpy as np
        HIDDEN = 512
        N_EXPERTS = 8
        N_SHARED = 2
        TOP_K = 2
        MOE_FF = 352
        SHARED_FF = N_SHARED * MOE_FF
        SCALE = 2.5
        BATCH, SEQ = (2, 256)
        key = jax.random.key(seed)
        ks = jax.random.split(key, 8)
        s = 0.02
        return {'hidden_states': jax.random.normal(ks[0], (BATCH, SEQ, HIDDEN), jnp.float32), 'gate_w': jax.random.normal(ks[1], (N_EXPERTS, HIDDEN), jnp.float32) * s, 'shared_wg': jax.random.normal(ks[2], (SHARED_FF, HIDDEN), jnp.float32) * s, 'shared_wu': jax.random.normal(ks[3], (SHARED_FF, HIDDEN), jnp.float32) * s, 'shared_wd': jax.random.normal(ks[4], (HIDDEN, SHARED_FF), jnp.float32) * s, 'exp_wg': jax.random.normal(ks[5], (N_EXPERTS, MOE_FF, HIDDEN), jnp.float32) * s, 'exp_wu': jax.random.normal(ks[6], (N_EXPERTS, MOE_FF, HIDDEN), jnp.float32) * s, 'exp_wd': jax.random.normal(ks[7], (N_EXPERTS, HIDDEN, MOE_FF), jnp.float32) * s}
    _L0_ffn_all = _L0_ffn_setup()
    _L0_ffn_in = {k: v for k, v in _L0_ffn_all.items() if k in ('gate_w', 'shared_wg', 'shared_wu', 'shared_wd', 'exp_wg', 'exp_wu', 'exp_wd')}
    del _L0_ffn_all
    return {'x': x, 'fside_S2_0': fside_S2_0, 'ctx_2048': ctx_2048, 'L0_xattn_k': _L0_xattn_in['k'], 'L0_ffn_gate_w': _L0_ffn_in['gate_w'], 'L0_ffn_shared_wg': _L0_ffn_in['shared_wg'], 'L0_ffn_shared_wu': _L0_ffn_in['shared_wu'], 'L0_ffn_shared_wd': _L0_ffn_in['shared_wd'], 'L0_ffn_exp_wg': _L0_ffn_in['exp_wg'], 'L0_ffn_exp_wu': _L0_ffn_in['exp_wu'], 'L0_ffn_exp_wd': _L0_ffn_in['exp_wd']}

def reference(x, fside_S2_0, ctx_2048, L0_xattn_k, L0_ffn_gate_w, L0_ffn_shared_wg, L0_ffn_shared_wu, L0_ffn_shared_wd, L0_ffn_exp_wg, L0_ffn_exp_wu, L0_ffn_exp_wd):
    import jax
    import jax.numpy as jnp

    def _L0_xattn_ref(v, k, bias, x1, x2, num_heads):
        import jax, jax.numpy as jnp
        import numpy as np
        B, D, L = v.shape
        H = D // num_heads
        fft_size = 2 * L
        vr = v.reshape(B, H, num_heads, L)
        x1r = x1.reshape(B, H, num_heads, L)
        x2r = x2.reshape(B, H, num_heads, L)
        kv = vr[:, :, :, None, :] * x2r[:, :, None, :, :]
        k_f = jnp.fft.rfft(k.astype(jnp.float32), n=fft_size)
        y = jnp.fft.irfft(jnp.fft.rfft(kv, n=fft_size) * k_f[None, :, None, None, :], n=fft_size)[..., :L]
        skip = bias.astype(jnp.float32).reshape(H, num_heads)[None, :, :, None, None]
        y = y + kv * skip
        out = jnp.einsum('bhijl,bhil->bhjl', y, x1r)
        return out.reshape(B, D, L)

    def _L0_ffn_ref(hidden_states, gate_w, shared_wg, shared_wu, shared_wd, exp_wg, exp_wu, exp_wd):
        import jax, jax.numpy as jnp
        import numpy as np
        HIDDEN = 512
        N_EXPERTS = 8
        N_SHARED = 2
        TOP_K = 2
        MOE_FF = 352
        SHARED_FF = N_SHARED * MOE_FF
        SCALE = 2.5
        BATCH, SEQ = (2, 256)
        B, S, D = hidden_states.shape
        T = B * S
        xf = hidden_states.reshape(T, D)
        scores = jax.nn.sigmoid(xf @ gate_w.T)
        topk_w, topk_idx = jax.lax.top_k(scores, TOP_K)
        topk_w = topk_w / (topk_w.sum(axis=-1, keepdims=True) + 1e-20)
        topk_w = topk_w * SCALE
        shared_out = jax.nn.silu(xf @ shared_wg.T) * (xf @ shared_wu.T) @ shared_wd.T
        h = jax.nn.silu(jnp.einsum('td,efd->etf', xf, exp_wg)) * jnp.einsum('td,efd->etf', xf, exp_wu)
        all_out = jnp.einsum('etf,edf->etd', h, exp_wd)
        picked = all_out[topk_idx, jnp.arange(T)[:, None]]
        routed_out = (topk_w[..., None] * picked).sum(axis=1)
        return (shared_out + routed_out).reshape(B, S, D)
    x = x + _L0_xattn_ref(_layernorm(x, axis=-1), L0_xattn_k, fside_S2_0, ctx_2048, ctx_2048, 8)
    x = x + _L0_ffn_ref(_layernorm(x, axis=-1), L0_ffn_gate_w, L0_ffn_shared_wg, L0_ffn_shared_wu, L0_ffn_shared_wd, L0_ffn_exp_wg, L0_ffn_exp_wu, L0_ffn_exp_wd)
    return x

_drawn_inputs = setup_inputs


def setup_inputs(seed=0):
    import zlib

    import numpy as np

    out = dict(_drawn_inputs(seed))
    spreads = {}
    factors = {'L0_ffn_gate_w': 5.244,
     'L0_ffn_shared_wg': 5.792,
     'L0_ffn_shared_wu': 5.672,
     'L0_ffn_shared_wd': 5.672,
     'L0_ffn_exp_wg': 4.618,
     'L0_ffn_exp_wu': 4.499,
     'L0_ffn_exp_wd': 4.514}
    for name, (base, spread) in spreads.items():
        noise = np.random.default_rng([zlib.crc32(name.encode()), seed]).standard_normal(out[name].shape)
        drawn = base * np.exp(spread * noise) if base else spread * noise
        out[name] = jnp.asarray(drawn.astype(out[name].dtype))
    for name, factor in factors.items():
        out[name] = (out[name] * factor).astype(out[name].dtype)
    return out
```

```python
from contextlib import ExitStack

import concourse.bass as bass
from concourse import mybir

ALU = mybir.AluOpType
ACT = mybir.ActivationFunctionType
AX_X = mybir.AxisListType.X
F32 = mybir.dt.float32
F16 = mybir.dt.float16
I32 = mybir.dt.int32
U32 = mybir.dt.uint32

P = 128
B, S, L = 8, 256, 512
NH = 8
H = S // NH
LB = L // P
HG = 8
G = H // HG
RG = HG * NH
TG = B * RG
Q = TG // P
T = B * S
COLS = B * NH * NH
E = 8
FF = 352
FK = -(-FF // P)
SFF = 704
SM = -(-SFF // P)
SFP = SM * P
SH_GU = LB * 2 * SFP
SH_W = SH_GU + SM * L
SH_PIECE = 1024
SH_PIECES = SH_W // SH_PIECE
EX_W = 2 * LB * FF + FK * L
EX_PARTS = 4
EX_PIECE = EX_W // EX_PARTS
TILES = 2 * T // P + E - 1
TROWS = E * T + E * P
RING = 4
EPS = 1e-5
ROUTE_SCALE = 2.5
WS = 256.0
SLOTS = -(-TILES // RING) * RING
CONST_W = 4 * P + 20 + SLOTS + Q
KREV = L + P


def xattn_moe(nc, x, ctx_in, skip, krev, gate_w, shared_w, expert_w, consts, table0, zeros, out):
    filters = bass.AP(krev.tensor, 0, [[KREV, H], [1, P], [1, L]])
    x_rows = x.rearrange("b (g r) l -> g b r l", r=RG)
    ctx_rows = ctx_in.rearrange("b (g r) l -> g b r l", r=RG)
    out_rows = out[0:T, :].rearrange("(b g r) l -> g b r l", b=B, g=G)
    xf_dram = nc.dram_tensor("normed_tokens", [T + P, L], F32).ap()
    xf_rows = xf_dram[0:T, :].rearrange("(b g r) l -> g b r l", b=B, g=G)
    table = nc.dram_tensor("pair_table", [TROWS, 2], I32).ap()

    with ExitStack() as stack:
        def sb(name, shape, dt):
            return stack.enter_context(nc.sbuf_tensor(name, shape, dt))

        def sem(name):
            return stack.enter_context(nc.semaphore(name))

        ps = stack.enter_context(nc.psum_tensor("banks", [P, 8, 512], F32))

        arena = sb("arena", [P, E * EX_W], F32)
        place = [0]

        def carve(words):
            place[0] += words
            return arena[:, place[0] - words:place[0]]

        kv = [carve(LB * COLS) for _ in range(2)]
        kvh = [carve(LB * COLS // 2).bitcast(F16) for _ in range(2)]
        kvl = [carve(LB * COLS // 2).bitcast(F16) for _ in range(2)]
        prod = carve(LB * COLS)
        vT = [carve(LB * TG) for _ in range(2)]
        cT = [carve(LB * TG) for _ in range(2)]
        filt_raw = [carve(L) for _ in range(2)]
        fh = [carve(L // 2).bitcast(F16) for _ in range(2)]
        fl = [carve(L // 2).bitcast(F16) for _ in range(2)]
        ctx_tok = carve(Q * L).rearrange("p (q l) -> p q l", q=Q)
        x_tok2 = carve(Q * L).rearrange("p (q l) -> p q l", q=Q)
        place[0] = E * EX_W - SH_W
        shared_gu = carve(SH_GU)
        shared_d = carve(SH_W - SH_GU)
        early_experts = (E * EX_W - SH_W) // EX_W
        gu_h, gu_l = shared_gu[:, 0:SH_GU // 2].bitcast(F16), shared_gu[:, SH_GU // 2:SH_GU].bitcast(F16)
        d_n = SH_W - SH_GU
        d_h, d_l = shared_d[:, 0:d_n // 2].bitcast(F16), shared_d[:, d_n // 2:d_n].bitcast(F16)
        experts = arena[:, :].bitcast(F16)

        x_tok = [sb(f"x_tok{i}", [P, Q, L], F32) for i in range(2)] + [x_tok2]
        normed = sb("normed", [P, Q, L], F32)
        mixT = sb("mixT", [P, LB * TG], F32)
        xfh = sb("xfh", [P, LB, TG], F16)
        xfl = sb("xfl", [P, LB, TG], F16)
        silu = sb("silu", [P, 512], F32)
        hm = sb("hm", [P, 512], F32)
        skipped = hm
        hTh = sb("hTh", [P, SM, TG], F16)
        hTl = sb("hTl", [P, SM, TG], F16)
        stage = [sb(f"stage{i}", [P, EX_PIECE], F32) for i in range(2)]
        con = sb("con", [P, CONST_W], F32)
        ident, block8, before, ones = (con[:, i * P:(i + 1) * P] for i in range(4))
        iota8 = con[:, 4 * P:4 * P + 8]
        minus_half = con[:, 4 * P + 8:4 * P + 12]
        first_row = con[:, 4 * P + 12:4 * P + 20]
        tile_no = con[0:1, 4 * P + 20:4 * P + 20 + SLOTS]
        row_base = con[:, 4 * P + 20 + SLOTS:CONST_W]
        tok_ids = sb("tok_ids", [P, Q], I32)
        skip_col = sb("skip_col", [P, G], F32)
        gate_raw = sb("gate_raw", [P, LB * E], F32)
        gate_h = sb("gate_h", [P, LB * E], F16)
        gate_l = sb("gate_l", [P, LB * E], F16)
        stats = sb("stats", [P, Q, 6], F32)
        meanvar = sb("meanvar", [P, Q, 2], F32)
        var_eps = sb("var_eps", [P, Q], F32)
        rstd = sb("rstd", [P, Q], F32)
        score = sb("score", [P, Q, E], F32)
        top = sb("top", [P, Q, E], F32)
        topi = sb("topi", [P, Q, E], U32)
        topf = sb("topf", [P, Q, 2], F32)
        onehot = sb("onehot", [P, Q, 2, E], F32)
        picked = sb("picked", [P, Q, E], F32)
        rank = sb("rank", [P, Q, E], F32)
        rankhot = sb("rankhot", [P, Q, 2, E], F32)
        rowf = sb("rowf", [P, Q, 2], F32)
        row = sb("row", [P, Q, 2], I32)
        pair = sb("pair", [P, Q, 2, 2], I32)
        wsum = sb("wsum", [P, Q], F32)
        winv = sb("winv", [P, Q], F32)
        wtop = sb("wtop", [P, Q, 2], F32)
        next_row = sb("next_row", [P, E], F32)
        n_i = sb("n_i", [1, E], I32)
        n_f = sb("n_f", [1, E], F32)
        n_end = sb("n_end", [1, E], F32)
        past, past_n = (mixT[0:1, i * L:i * L + SLOTS * E].rearrange("p (t e) -> p t e", e=E) for i in range(2))
        t_exp = sb("t_exp", [1, SLOTS], F32)
        t_start = sb("t_start", [1, SLOTS], F32)
        t_row = sb("t_row", [1, SLOTS], F32)
        tile_row = sb("tile_row", [1, SLOTS], I32)
        tile_w = sb("tile_w", [1, SLOTS], I32)
        ids = [sb(f"ids{i}", [P, 2], I32) for i in range(RING)]
        xg = [mixT[:, i * L:(i + 1) * L] for i in range(2)]
        yg = [mixT[:, (2 + i) * L:(3 + i) * L] for i in range(2)]
        xgh = [xfh[:, i, :] for i in range(2)]
        xgl = [xfl[:, i, :] for i in range(2)]
        hgh = xfh[:, 2, 0:FK * P]
        hgl = xfl[:, 2, 0:FK * P]

        const_in = sem("const_in")
        tok_in = [sem(f"tok_in{g}") for g in range(G)]
        filt_in = [sem(f"filt_in{i}") for i in range(2)]
        stage_in = [sem(f"stage_in{i}") for i in range(2)]
        init_done = sem("init_done")
        base_stored = sem("base_stored")
        xf_stored = sem("xf_stored")
        pairs_stored = sem("pairs_stored")
        ids_in = [sem(f"ids_in{i}") for i in range(RING)]
        gathered = [sem(f"gathered{i}") for i in range(2)]
        added = sem("added")
        kv_ready = sem("kv_ready")
        kvh_ready = sem("kvh_ready")
        kvl_ready = sem("kvl_ready")
        conv_ready = sem("conv_ready")
        prod_done = sem("prod_done")
        mix_done = sem("mix_done")
        v_ready = sem("v_ready")
        skip_ready = sem("skip_ready")
        tokT_ready = sem("tokT_ready")
        tokT_done = sem("tokT_done")
        skipsum_ready = sem("skipsum_ready")
        skip_done = sem("skip_done")
        var_ready = sem("var_ready")
        rstd_ready = sem("rstd_ready")
        outT_ready = sem("outT_ready")
        x1_done = sem("x1_done")
        xf_ready = sem("xf_ready")
        xfT_ready = sem("xfT_ready")
        xfh_ready = sem("xfh_ready")
        xfl_ready = sem("xfl_ready")
        logit_ready = sem("logit_ready")
        score_ready = sem("score_ready")
        picked_ready = sem("picked_ready")
        rank_ready = sem("rank_ready")
        rank_used = sem("rank_used")
        pair_ready = sem("pair_ready")
        gu_ready = sem("gu_ready")
        silu_ready = sem("silu_ready")
        hm_done = sem("hm_done")
        hh_ready = sem("hh_ready")
        hl_ready = sem("hl_ready")
        down_ready = sem("down_ready")
        base_ready = sem("base_ready")
        piece_h = sem("piece_h")
        piece_l = sem("piece_l")
        gate_split_h = sem("gate_split_h")
        gate_split_l = sem("gate_split_l")
        tiles_ready = sem("tiles_ready")
        dve_step = sem("dve_step")
        pool_passed = sem("pool_passed")
        r_gu = sem("r_gu")
        r_silu = sem("r_silu")
        r_hm = sem("r_hm")
        r_xT = sem("r_xT")
        r_xh = sem("r_xh")
        r_xl = sem("r_xl")
        r_hT = sem("r_hT")
        r_hh = sem("r_hh")
        r_hl = sem("r_hl")
        r_down = sem("r_down")
        r_y = sem("r_y")

        bank = [ps[:, i, :] for i in range(8)]
        GATE, UP = bank[4], bank[5]

        def turns_of(name, g):
            if name == "prep":
                for q in range(Q):
                    yield tokT_done, 2 * (Q * g + q) + 1
                    yield tokT_done, 2 * (Q * g + q) + 2
                    yield skip_done, Q * g + q + 1
            elif name == "out":
                for q in range(Q):
                    yield x1_done, Q * g + q + 1
            elif name == "xf":
                for q in range(Q):
                    yield xfl_ready, Q * g + q + 1
                yield score_ready, g + 1
            elif name == "rank":
                yield rank_used, g + 1

        turn_order = [("prep", 0)]
        for g in range(G):
            turn_order += [("xf", g - 1), ("rank", g - 1)] if g > 0 else []
            turn_order += [("prep", g + 1)] if g < G - 1 else []
            turn_order += [("out", g)]
        turn_order += [("xf", G - 1), ("rank", G - 1)]
        turn_read = [t for name, g in turn_order for t in turns_of(name, g)]

        def turn_bank(name, g, k):
            n = sum(len(list(turns_of(*w))) for w in turn_order[:turn_order.index((name, g))])
            return bank[6 + (n + k) % 2]

        def backwards(v):
            return bass.AP(v.tensor, v.offset + L - 1, [v.ap[0], [-1, L]])

        def heads(v):
            return v.rearrange("p (a r) -> p a r", r=RG)

        block = stack.enter_context(nc.Block())


        @block.sync
        def _(sp):
            def load_filter(s, par):
                sp.dma_start(filt_raw[par], filters[bass.ds(s, 1), :, :].rearrange("o p l -> (o p) l")
                             ).then_inc(filt_in[par], 16)

            def next_filter(s, par):
                sp.wait_ge(kvl_ready, s - 1)
                load_filter(s, par)

            def load_tokens(g):
                for b2 in range(2):
                    rows = slice(b2 * RG, (b2 + 1) * RG)
                    sp.dma_start(ctx_tok[rows, :, :], ctx_rows[g].rearrange("(q t) r l -> t r q l", t=2)[b2]
                                 ).then_inc(tok_in[g], 16)
                    sp.dma_start(x_tok[g % 3][rows, :, :], x_rows[g].rearrange("(q t) r l -> t r q l", t=2)[b2]
                                 ).then_inc(tok_in[g], 16)

            def store(dst, src, done):
                for b2 in range(2):
                    sp.dma_start(dst.rearrange("(q t) r l -> t r q l", t=2)[b2],
                                 src[b2 * RG:(b2 + 1) * RG, :, :]).then_inc(done, 16)

            def load_shared(i, par):
                sp.dma_start(stage[par][:, 0:SH_PIECE], shared_w[:, bass.ds(i * SH_PIECE, SH_PIECE)]
                             ).then_inc(stage_in[par], 16)

            def next_shared(i, par):
                sp.wait_ge(piece_l, i - 1)
                load_shared(i, par)

            def load_expert(e):
                for c in range(EX_PARTS):
                    par = (SH_PIECES + c) % 2
                    sp.wait_ge(piece_l, SH_PIECES - 1 + e * EX_PARTS + c)
                    sp.dma_start(stage[par][:], expert_w[bass.ds(e, 1), :, c * EX_PIECE:(c + 1) * EX_PIECE]
                                 .rearrange("e p n -> (e p) n")).then_inc(stage_in[par], 16)

            load_tokens(0)
            sp.dma_start(con[:], consts).then_inc(const_in, 16)
            sp.dma_start(skip_col[:], skip).then_inc(const_in, 16)
            sp.dma_start(gate_raw[:], gate_w).then_inc(const_in, 16)
            load_filter(0, 0)
            load_filter(1, 1)
            load_shared(0, 0)
            load_shared(1, 1)
            sp.dma_start(table, table0).then_inc(init_done, 16)
            sp.dma_start(xf_dram[T:T + P, :], zeros).then_inc(init_done, 16)
            sp.dma_start(out[T:T + P, :], zeros).then_inc(init_done, 16)
            for g in range(G):
                s0 = g * HG
                if g < G - 1:
                    sp.wait_ge(skip_done, Q * (g + 1))
                    if g >= 2:
                        sp.wait_ge(base_stored, 32 * (g - 1))
                    load_tokens(g + 1)
                next_filter(s0 + 2, 0)
                if g == 0:
                    next_shared(2, 0)
                else:
                    sp.wait_ge(xf_ready, Q * g)
                    store(xf_rows[g - 1], normed, xf_stored)
                pairs = 3 if g < G - 1 else 2
                with sp.Fori(0, pairs) as j:
                    for u in range(2):
                        next_filter(s0 + 3 + 2 * j + u, (1 + u) % 2)
                        if g == 0:
                            next_shared(3 + 2 * j + u, (1 + u) % 2)
                next_filter(s0 + 3 + 2 * pairs, 1)
                if g > 0:
                    sp.wait_ge(base_ready, Q * g)
                    store(out_rows[g - 1], x_tok[(g - 1) % 3], base_stored)
            sp.wait_ge(xf_ready, Q * G)
            store(xf_rows[G - 1], normed, xf_stored)
            with sp.Fori(0, E - 1) as e:
                load_expert(e)
            sp.wait_ge(base_ready, Q * G)
            store(out_rows[G - 1], x_tok[(G - 1) % 3], base_stored)
            load_expert(E - 1)

            def load_ids(t, slot):
                r = sp.value_load(tile_row[0:1, bass.ds(t, 1)], min_val=0, max_val=TROWS - P)
                sp.dma_start(ids[slot][:], table[bass.ds(r, P), :]).then_inc(ids_in[slot], 16)

            sp.wait_ge(tiles_ready, 1)
            sp.wait_ge(pairs_stored, 16 * G * Q * 2)
            for t in range(RING):
                load_ids(t, t)
            with sp.Fori(0, TILES // RING - 1) as j:
                for u in range(RING):
                    sp.wait_ge(added, 16 * (j * RING + u + 1))
                    load_ids(RING + j * RING + u, u)
            for t in range(TILES // RING * RING, TILES):
                sp.wait_ge(added, 16 * (t - RING + 1))
                load_ids(t, t % RING)
            sp.wait_ge(base_stored, 32 * G)
            sp.wait_ge(xf_stored, 32 * G)
            sp.wait_ge(init_done, 48)
            sp.wait_ge(added, 16 * TILES)

        @block.gpsimd
        def _(pool):
            def outer(s, h, g, par):
                v = heads(vT[g % 2])[:, :, bass.ds(h * NH, NH)]
                c = heads(cT[g % 2])[:, :, bass.ds(h * NH, NH)]
                shape = [P, LB * B, NH, NH]
                nc.gpsimd.tensor_tensor(kv[par].rearrange("p (a i j) -> p a i j", i=NH, j=NH),
                                        v[:, :, :, None].to_broadcast(shape), c[:, :, None, :].to_broadcast(shape),
                                        ALU.mult).then_inc(kv_ready, 1)

            def inverse_root(n):
                pool.wait_ge(var_ready, n + 1)
                nc.gpsimd.tensor_tensor(rstd[:], var_eps[:], minus_half, ALU.pow).then_inc(rstd_ready, 1)

            def store_pairs(g):
                pool.wait_ge(pair_ready, g + 1)
                for q in range(Q):
                    for k in range(2):
                        nc.gpsimd.indirect_dma_start(
                            out=table, out_offset=bass.IndirectOffsetOnAxis(ap=row[:, q, k:k + 1], axis=0),
                            in_=pair[:, q, k, :], in_offset=None).then_inc(pairs_stored, 16)

            pool.wait_ge(const_in, 48)
            inverse_root(0)
            pool.wait_ge(tokT_done, 2 * Q)
            outer(0, 0, 0, 0)
            pool.wait_ge(init_done, 48)
            for g in range(G):
                s0 = g * HG
                if g == 0:
                    outer(s0 + 1, 1, g, 1)
                else:
                    pool.wait_ge(kvl_ready, s0)
                    outer(s0 + 1, 1, g, 1)
                if g < G - 1:
                    inverse_root(2 * g + 1)
                with pool.Fori(0, 3) as j:
                    for u in range(2):
                        pool.wait_ge(kvl_ready, s0 + 2 * j + u + 1)
                        outer(s0 + 2 + 2 * j + u, 2 + 2 * j + u, g, u)
                if g < G - 1:
                    pool.wait_ge(tokT_done, 2 * Q * (g + 2))
                    pool.wait_ge(kvl_ready, s0 + HG - 1)
                    outer(s0 + HG, 0, g + 1, 0)
                inverse_root(2 * g + 2 if g < G - 1 else 2 * G - 1)
                if g > 0:
                    store_pairs(g - 1)
            store_pairs(G - 1)

            def gather(slot, par, n):
                pool.wait_ge(ids_in[slot], 16 * n)
                pool.sem_inc(pool_passed, 1)
                pool.wait_ge(xf_stored, 32 * G)
                nc.gpsimd.indirect_dma_start(
                    out=xg[par], out_offset=None, in_=xf_dram,
                    in_offset=bass.IndirectOffsetOnAxis(ap=ids[slot][:, 0:1], axis=0)).then_inc(gathered[par], 16)

            def add_tile(t, slot, par):
                pool.wait_ge(r_y, t + 1)
                if not isinstance(t, int) or t > 0:
                    pool.wait_ge(added, 16 * t)
                pool.sem_inc(pool_passed, 1)
                pool.wait_ge(base_stored, 32 * G)
                nc.gpsimd.indirect_dma_start(
                    out=out, out_offset=bass.IndirectOffsetOnAxis(ap=ids[slot][:, 0:1], axis=0),
                    in_=yg[par], in_offset=None, compute_op=ALU.add).then_inc(added, 16)

            pool.wait_ge(outT_ready, Q * G)
            gather(0, 0, 1)
            gather(1, 1, 1)
            pool.wait_ge(r_xT, 1)
            gather(2, 0, 1)
            add_tile(0, 0, 0)
            with pool.Fori(0, (TILES - 3) // RING) as j:
                for u in range(1, RING + 1):
                    pool.wait_ge(r_xT, RING * j + u + 1)
                    gather((u + 2) % RING, u % 2, j + 1 + (u + 2) // RING)
                    add_tile(RING * j + u, u % RING, u % 2)
            for t in range(TILES - 2, TILES):
                add_tile(t, t % RING, t % 2)

        @block.tensor
        def _(pe):
            turn = [0]

            def take():
                k = turn[0]
                turn[0] += 1
                if k >= 2:
                    pe.wait_ge(*turn_read[k - 2])
                return bank[6 + k % 2]

            def split_products(dst, w, x, n):
                for k in range(n):
                    (wh, wl), (xh, xl) = w(k), x(k)
                    nc.tensor.matmul(dst, wh, xh, start=(k == 0), stop=False)
                    nc.tensor.matmul(dst, wh, xl, start=False, stop=False)
                    last = nc.tensor.matmul(dst, wl, xh, start=False, stop=(k == n - 1))
                return last

            def convolve(s, par, first=False):
                pe.wait_ge(kvl_ready, s + 1)
                for n in range(LB):
                    if not first:
                        pe.wait_ge(prod_done, LB * s - LB + 1 + n)
                    last = split_products(
                        bank[n],
                        lambda m: (fh[par][:, (n - m) * P:(n - m + 1) * P], fl[par][:, (n - m) * P:(n - m + 1) * P]),
                        lambda m: (kvh[par][:, m * COLS:(m + 1) * COLS], kvl[par][:, m * COLS:(m + 1) * COLS]), n + 1)
                    last.then_inc(conv_ready, 1)

            def transpose_tile(dst, src, done):
                for lb in range(LB):
                    last = nc.tensor.transpose(dst[:, lb * P:(lb + 1) * P], src(lb), ident)
                last.then_inc(done, 1)

            def prepare(g, q):
                if q == 0:
                    pe.wait_ge(tok_in[g], 64)
                transpose_tile(take(), lambda lb: ctx_tok[:, q, lb * P:(lb + 1) * P], tokT_ready)
                t = take()
                pe.wait_ge(v_ready, Q * g + q + 1)
                transpose_tile(t, lambda lb: normed[:, q, lb * P:(lb + 1) * P], tokT_ready)
                t = take()
                pe.wait_ge(skip_ready, Q * g + q + 1)
                nc.tensor.matmul(t, block8, skipped[:], start=True, stop=True).then_inc(skipsum_ready, 1)

            def mix_out(g):
                pe.wait_ge(mix_done, HG * (g + 1))
                for q in range(Q):
                    transpose_tile(take(), lambda lb: mixT[:, lb * TG + q * P:lb * TG + (q + 1) * P], outT_ready)

            def normed_out(g):
                for q in range(Q):
                    t = take()
                    pe.wait_ge(xf_ready, Q * g + q + 1)
                    transpose_tile(t, lambda lb: normed[:, q, lb * P:(lb + 1) * P], xfT_ready)
                t = take()
                pe.wait_ge(xfl_ready, Q * (g + 1))
                pe.wait_ge(gate_split_l, 1)
                for q in range(Q):
                    last = split_products(
                        t[:, q * E:(q + 1) * E],
                        lambda lb: (xfh[:, lb, q * P:(q + 1) * P], xfl[:, lb, q * P:(q + 1) * P]),
                        lambda lb: (gate_h[:, lb * E:(lb + 1) * E], gate_l[:, lb * E:(lb + 1) * E]), LB)
                last.then_inc(logit_ready, 1)

            def ranks(g):
                t = take()
                pe.wait_ge(picked_ready, g + 1)
                for q in range(Q + 1):
                    for k in range(q):
                        last = nc.tensor.matmul(t[:, q * E:(q + 1) * E], ones, picked[:, k, :],
                                                start=(k == 0), stop=(k == Q - 1))
                    if q < Q:
                        nc.tensor.matmul(t[:, q * E:(q + 1) * E], before, picked[:, q, :], start=(q == 0), stop=True)
                last.then_inc(rank_ready, 1)

            def gate_up(g, m):
                pe.wait_ge(hm_done, SM * g + m + 1)
                if g > 0:
                    pe.wait_ge(base_ready, Q * g)
                for half, dst in ((0, GATE), (1, UP)):
                    last = split_products(
                        dst,
                        lambda lb: (gu_h[:, bass.ds((2 * lb + half) * SFP + m * P, P)],
                                    gu_l[:, bass.ds((2 * lb + half) * SFP + m * P, P)]),
                        lambda lb: (xfh[:, lb, :], xfl[:, lb, :]), LB)
                last.then_inc(gu_ready, 1)

            def down(g, q):
                if q == 0:
                    pe.wait_ge(hl_ready, SM * (g + 1))
                if q >= 2:
                    pe.wait_ge(base_ready, Q * g + q - 1)
                last = split_products(
                    bank[4 + q % 2],
                    lambda k: (hTh[:, k, q * P:(q + 1) * P], hTl[:, k, q * P:(q + 1) * P]),
                    lambda k: (d_h[:, k * L:(k + 1) * L], d_l[:, k * L:(k + 1) * L]), SM)
                last.then_inc(down_ready, 1)

            pe.wait_ge(const_in, 48)
            for q in range(Q):
                prepare(0, q)
            for g in range(G):
                s0 = g * HG
                convolve(s0, 0, first=(g == 0))
                if g == 1:
                    pe.wait_ge(piece_l, SH_PIECES)
                if g > 0:
                    normed_out(g - 1)
                with pe.Fori(0, 3) as j:
                    for u in range(2):
                        convolve(s0 + 1 + 2 * j + u, (1 + u) % 2)
                        if g > 0:
                            gate_up(g - 1, 2 * j + u)
                if g > 0:
                    ranks(g - 1)
                for q in range(Q):
                    if g < G - 1:
                        prepare(g + 1, q)
                    if g > 0:
                        down(g - 1, q)
                convolve(s0 + HG - 1, 1)
                mix_out(g)
            normed_out(G - 1)
            with pe.Fori(0, early_experts) as m:
                gate_up(G - 1, m)
            for m in range(early_experts, SM):
                gate_up(G - 1, m)
            ranks(G - 1)
            for q in range(Q):
                down(G - 1, q)

            def tile_in(t, par, n):
                pe.wait_ge(gathered[par], n)
                transpose_tile(bank[2], lambda lb: xg[par][:, lb * P:(lb + 1) * P], r_xT)

            def tile_gate_up(t, par, w):
                pe.wait_ge(r_xl, t + 1)
                for half in range(2):
                    last = split_products(
                        bank[half][:, 0:FF],
                        lambda lb: (xgh[par][:, lb * P:(lb + 1) * P], xgl[par][:, lb * P:(lb + 1) * P]),
                        lambda lb: (experts[:, bass.ds(w + (half * LB + lb) * FF, FF)],
                                    experts[:, bass.ds(w + EX_W + (half * LB + lb) * FF, FF)]), LB)
                last.then_inc(r_gu, 1)

            def tile_hidden(t):
                pe.wait_ge(r_hm, t + 1)
                for k in range(FK):
                    c = min(k * P, FF - P)
                    last = nc.tensor.transpose(bank[3][:, k * P:(k + 1) * P], hm[:, c:c + P], ident)
                last.then_inc(r_hT, 1)

            def tile_down(t, w):
                pe.wait_ge(r_hl, t + 1)
                if not isinstance(t, int) or t > 0:
                    pe.wait_ge(r_y, t)
                last = split_products(
                    bank[4],
                    lambda k: (hgh[:, k * P:(k + 1) * P], hgl[:, k * P:(k + 1) * P]),
                    lambda k: (experts[:, bass.ds(w + 2 * LB * FF + k * L, L)],
                               experts[:, bass.ds(w + EX_W + 2 * LB * FF + k * L, L)]), FK)
                last.then_inc(r_down, 1)

            def weights_of(t):
                return pe.value_load(tile_w[0:1, bass.ds(t, 1)], min_val=0, max_val=(E - 1) * 2 * EX_W)

            pe.wait_ge(tiles_ready, 1)
            pe.wait_ge(piece_l, SH_PIECES + E * EX_PARTS)
            pe.wait_ge(base_ready, Q * G)
            pe.wait_ge(prod_done, LB * H)
            tile_in(0, 0, 16)
            tile_gate_up(0, 0, weights_of(0))
            tile_in(1, 1, 16)
            tile_hidden(0)
            for t in range(1, RING + 1):
                tile_gate_up(t, t % 2, weights_of(t))
                tile_in(t + 1, (t + 1) % 2, 16 * ((t + 1) // 2 + 1))
                tile_down(t - 1, weights_of(t - 1))
                tile_hidden(t)
            with pe.Fori(1, (TILES - 3) // RING) as j:
                for u in range(1, RING + 1):
                    t = RING * j + u
                    tile_gate_up(t, u % 2, weights_of(t))
                    tile_in(t + 1, (u + 1) % 2, 32 * j + 16 * ((u + 1) // 2 + 1))
                    tile_down(t - 1, weights_of(t - 1))
                    tile_hidden(t)
            for t in range(TILES - 2, TILES):
                tile_gate_up(t, t % 2, weights_of(t))
                if t + 1 < TILES:
                    tile_in(t + 1, (t + 1) % 2, 16 * ((t + 1) // 2 + 1))
                tile_down(t - 1, weights_of(t - 1))
                tile_hidden(t)
            tile_down(TILES - 1, weights_of(TILES - 1))

        @block.scalar
        def _(act):
            def high_parts(s, par, n, reuse=True):
                act.wait_ge(filt_in[par], 16 * n)
                if reuse:
                    act.wait_ge(conv_ready, LB * s - LB)
                nc.scalar.activation(fh[par], backwards(filt_raw[par]), ACT.Copy, scale=WS)
                act.wait_ge(kv_ready, s + 1)
                nc.scalar.activation(kvh[par], kv[par], ACT.Copy).then_inc(kvh_ready, 1)

            def turned(g):
                if g >= 2:
                    act.wait_ge(mix_done, HG * (g - 1))
                for q in range(Q):
                    for k, dst in enumerate((cT[g % 2], vT[g % 2])):
                        act.wait_ge(tokT_ready, 2 * (Q * g + q) + k + 1)
                        nc.scalar.copy(dst.rearrange("p (a t) -> p a t", a=LB)[:, :, q * P:(q + 1) * P],
                                       turn_bank("prep", g, 3 * q + k).rearrange("p (a t) -> p a t", a=LB)
                                       ).then_inc(tokT_done, 1)

            def normed_high(g):
                if g > 0:
                    act.wait_ge(gu_ready, SM * g)
                for q in range(Q):
                    act.wait_ge(xfT_ready, Q * g + q + 1)
                    nc.scalar.copy(xfh[:, :, q * P:(q + 1) * P],
                                   turn_bank("xf", g, q).rearrange("p (a t) -> p a t", a=LB)).then_inc(xfh_ready, 1)
                act.wait_ge(logit_ready, g + 1)
                nc.scalar.activation(score[:], turn_bank("xf", g, Q)[:, 0:Q * E].rearrange("p (q e) -> p q e", e=E),
                                     ACT.Sigmoid, scale=1 / WS).then_inc(score_ready, 1)

            def gated(g, m):
                act.wait_ge(gu_ready, SM * g + m + 1)
                nc.scalar.activation(silu[:], GATE, ACT.Silu, scale=1 / WS).then_inc(silu_ready, 1)
                act.wait_ge(hm_done, SM * g + m + 2)
                if g > 0:
                    act.wait_ge(down_ready, Q * g)
                nc.scalar.copy(hTh[:, bass.ds(m, 1), :].rearrange("p o t -> p (o t)"), hm[:]).then_inc(hh_ready, 1)

            def piece(dst, par, n, width):
                act.wait_ge(stage_in[par], 16 * n)
                nc.scalar.activation(dst, stage[par][:, 0:width], ACT.Copy, scale=WS).then_inc(piece_h, 1)

            def expert(e):
                for c in range(EX_PARTS):
                    i = SH_PIECES + c
                    piece(experts[:, bass.ds(e * (2 * EX_W) + c * EX_PIECE, EX_PIECE)], i % 2,
                          i // 2 + 1 + e * (EX_PARTS // 2), EX_PIECE)

            act.wait_ge(const_in, 48)
            nc.scalar.activation(gate_h[:], gate_raw[:], ACT.Copy, scale=WS).then_inc(gate_split_h, 1)
            turned(0)
            high_parts(0, 0, 1, reuse=False)
            for g in range(G):
                s0 = g * HG
                high_parts(s0 + 1, 1, s0 // 2 + 1, reuse=(g > 0))
                if g == 0:
                    for i in range(3):
                        piece(d_h[:, i * SH_PIECE:(i + 1) * SH_PIECE], i % 2, i // 2 + 1, SH_PIECE)
                else:
                    normed_high(g - 1)
                with act.Fori(0, 3) as j:
                    for u in range(2):
                        high_parts(s0 + 2 + 2 * j + u, u, s0 // 2 + 2 + j)
                        if g == 0:
                            piece(gu_h[:, bass.ds((2 * j + u) * SH_PIECE, SH_PIECE)], (1 + u) % 2, j + 2 + u, SH_PIECE)
                        else:
                            gated(g - 1, 2 * j + u)
                if g < G - 1:
                    turned(g + 1)
                    high_parts(s0 + HG, 0, s0 // 2 + HG // 2 + 1)
            normed_high(G - 1)
            act.wait_ge(mix_done, H)
            with act.Fori(0, early_experts) as m:
                gated(G - 1, m)
                expert(m)
            for m in range(early_experts, SM):
                gated(G - 1, m)
            act.wait_ge(base_stored, 32 * (G - 1))
            for e in range(early_experts, E):
                if e == E - 1:
                    act.wait_ge(down_ready, Q * G)
                expert(e)

            def tile_high(t, par):
                act.wait_ge(r_xT, t + 1)
                nc.scalar.copy(xgh[par], bank[2]).then_inc(r_xh, 1)

            def tile_silu(t):
                act.wait_ge(r_gu, t + 1)
                nc.scalar.activation(silu[:, 0:FF], bank[0][:, 0:FF], ACT.Silu, scale=1 / WS).then_inc(r_silu, 1)

            def tile_out(t, slot, par):
                act.wait_ge(r_down, t + 1)
                if not isinstance(t, int) or t >= 2:
                    act.wait_ge(added, 16 * (t - 1))
                nc.scalar.activation(yg[par], bank[4], ACT.Copy, scale=ids[slot][:, 1:2].bitcast(F32)
                                     ).then_inc(r_y, 1)

            def tile_hidden_high(t):
                act.wait_ge(r_hT, t + 1)
                nc.scalar.copy(hgh, bank[3][:, 0:FK * P]).then_inc(r_hh, 1)

            tile_high(0, 0)
            tile_silu(0)
            tile_high(1, 1)
            tile_hidden_high(0)
            for t in range(1, RING + 1):
                tile_silu(t)
                tile_high(t + 1, (t + 1) % 2)
                tile_out(t - 1, (t - 1) % RING, (t - 1) % 2)
                tile_hidden_high(t)
            with act.Fori(1, (TILES - 3) // RING) as j:
                for u in range(1, RING + 1):
                    t = RING * j + u
                    tile_silu(t)
                    tile_high(t + 1, (u + 1) % 2)
                    tile_out(t - 1, (u - 1) % RING, (u - 1) % 2)
                    tile_hidden_high(t)
            for t in range(TILES - 2, TILES):
                tile_silu(t)
                if t + 1 < TILES:
                    tile_high(t + 1, (t + 1) % 2)
                tile_out(t - 1, (t - 1) % RING, (t - 1) % 2)
                tile_hidden_high(t)
            tile_out(TILES - 1, (TILES - 1) % RING, (TILES - 1) % 2)

        @block.vector
        def _(dve):
            steps = [0]

            def link(*ins):
                for i in ins:
                    i.then_inc(dve_step, 1)
                    steps[0] += 1
                dve.wait_ge(dve_step, steps[0])

            def low_parts(s, par):
                dve.wait_ge(kvh_ready, s + 1)
                nc.vector.scalar_tensor_tensor(out=fl[par], in0=backwards(filt_raw[par]), scalar=WS, in1=fh[par],
                                               op0=ALU.mult, op1=ALU.subtract)
                nc.vector.tensor_tensor(kvl[par], kv[par], kvh[par], ALU.subtract).then_inc(kvl_ready, 1)

            def finish(s, h, g):
                if not isinstance(s, int) or s > 0:
                    dve.wait_ge(mix_done, s)
                for n in range(LB):
                    dve.wait_ge(conv_ready, LB * s + n + 1)
                    c = heads(cT[g % 2])[:, n * B:(n + 1) * B, bass.ds(h * NH, NH)]
                    nc.vector.tensor_tensor(
                        prod[:, n * COLS:(n + 1) * COLS].rearrange("p (b i j) -> p b i j", i=NH, j=NH),
                        bank[n].rearrange("p (b i j) -> p b i j", i=NH, j=NH),
                        c[:, :, :, None].to_broadcast([P, B, NH, NH]), ALU.mult).then_inc(prod_done, 1)
                dve.wait_ge(prod_done, LB * s + LB)
                nc.vector.tensor_reduce(heads(mixT)[:, :, bass.ds(h * NH, NH)],
                                        prod.rearrange("p (a i j) -> p a j i", i=NH, j=NH), AX_X, ALU.add
                                        ).then_inc(mix_done, 1)

            def moments(src, n):
                link(*[nc.vector.bn_stats(stats[:, q, :], src[:, q, :]) for q in range(Q)])
                link(*[nc.vector.bn_aggr(meanvar[:, q, :], stats[:, q, :]) for q in range(Q)])
                nc.vector.tensor_scalar(var_eps[:], meanvar[:, :, 1], EPS, None, ALU.add).then_inc(var_ready, 1)
                dve.wait_ge(rstd_ready, n + 1)

            def normalise(src, done):
                for q in range(Q):
                    nc.vector.tensor_scalar(normed[:, q, :], src[:, q, :], meanvar[:, q, 0:1], rstd[:, q:q + 1],
                                            ALU.subtract, ALU.mult).then_inc(done, 1)

            def values(g):
                dve.wait_ge(tok_in[g], 64)
                if g >= 2:
                    dve.wait_ge(xf_stored, 32 * (g - 1))
                moments(x_tok[g % 3], 0 if g == 0 else 2 * g - 1)
                if g >= 2:
                    dve.wait_ge(xfT_ready, Q * (g - 1))
                normalise(x_tok[g % 3], v_ready)

            def skip_product(g, q):
                if q > 0:
                    dve.wait_ge(skipsum_ready, Q * g + q)
                dve.wait_ge(v_ready, Q * g + q + 1)
                nc.vector.scalar_tensor_tensor(out=skipped[:], in0=ctx_tok[:, q, :], scalar=skip_col[:, g:g + 1],
                                               in1=normed[:, q, :], op0=ALU.mult, op1=ALU.mult).then_inc(skip_ready, 1)

            def skip_term(g, q):
                dve.wait_ge(skipsum_ready, Q * g + q + 1)
                if q + 1 < Q:
                    skip_product(g, q + 1)
                c, r = ctx_tok[:, q, :], x_tok[g % 3][:, q, :]
                dve.wait_ge(tokT_done, 2 * (Q * g + q) + 1)
                t = nc.vector.tensor_tensor(c, turn_bank("prep", g, 3 * q + 2), c, ALU.mult)
                link(t)
                nc.vector.tensor_tensor(r, r, c, ALU.add).then_inc(skip_done, 1)

            def normed_low(g):
                for q in range(Q):
                    dve.wait_ge(xfh_ready, Q * g + q + 1)
                    c = slice(q * P, (q + 1) * P)
                    nc.vector.tensor_tensor(xfl[:, :, c], turn_bank("xf", g, q).rearrange("p (a t) -> p a t", a=LB),
                                            xfh[:, :, c], ALU.subtract).then_inc(xfl_ready, 1)

            def pick(g):
                dve.wait_ge(score_ready, g + 1)
                link(*[nc.vector.max(top[:, q, :], score[:, q, :]) for q in range(Q)])
                link(*[nc.vector.max_index(topi[:, q, :], top[:, q, :], score[:, q, :]) for q in range(Q)])
                link(nc.vector.tensor_copy(topf[:], topi[:, :, 0:2]))
                shape = [P, Q, 2, E]
                for k in range(2):
                    shape = [P, Q, E]
                    i = nc.vector.tensor_tensor(onehot[:, :, k, :], iota8[:, None, :].to_broadcast(shape),
                                                topf[:, :, k:k + 1].to_broadcast(shape), ALU.is_equal)
                    link(i)
                nc.vector.tensor_tensor(picked[:], onehot[:, :, 0, :], onehot[:, :, 1, :], ALU.add
                                        ).then_inc(picked_ready, 1)

            def pairs(g):
                t = turn_bank("rank", g, 0)
                if g > 0:
                    dve.wait_ge(pairs_stored, 16 * 2 * Q * g)
                dve.wait_ge(rank_ready, g + 1)
                link(nc.vector.tensor_tensor(rank[:], t[:, 0:Q * E].rearrange("p (q e) -> p q e", e=E),
                                             next_row[:, None, :].to_broadcast([P, Q, E]), ALU.add))
                nc.vector.tensor_tensor(next_row[:], next_row[:], t[:, Q * E:(Q + 1) * E], ALU.add
                                        ).then_inc(rank_used, 1)
                for k in range(2):
                    i = nc.vector.tensor_tensor(rankhot[:, :, k, :], onehot[:, :, k, :], rank[:], ALU.mult)
                    link(i)
                link(nc.vector.tensor_reduce(rowf[:], rankhot[:], AX_X, ALU.add))
                link(nc.vector.tensor_copy(row[:], rowf[:]),
                     nc.vector.tensor_scalar(tok_ids[:], row_base, float(RG * g), None, ALU.add),
                     nc.vector.tensor_tensor(wsum[:], top[:, :, 0], top[:, :, 1], ALU.add))
                link(nc.vector.tensor_scalar(wsum[:], wsum[:], 1e-20, None, ALU.add))
                link(nc.vector.reciprocal(winv[:], wsum[:]))
                link(nc.vector.tensor_tensor(wtop[:], top[:, :, 0:2], winv[:, :, None].to_broadcast([P, Q, 2]), ALU.mult))
                link(nc.vector.tensor_scalar(pair[:, :, :, 1].bitcast(F32), wtop[:], ROUTE_SCALE / WS, None, ALU.mult),
                     nc.vector.tensor_copy(pair[:, :, 0, 0], tok_ids[:]))
                nc.vector.tensor_copy(pair[:, :, 1, 0], tok_ids[:]).then_inc(pair_ready, 1)

            def tile_table():
                dve.wait_ge(rank_used, G)
                link(nc.vector.tensor_tensor(n_f[:], next_row[0:1, :], first_row[0:1, :], ALU.subtract))
                link(nc.vector.tensor_scalar(n_i[:], n_f[:], float(P - 1), None, ALU.add))
                link(nc.vector.tensor_scalar(n_i[:], n_i[:], P.bit_length() - 1, None, ALU.arith_shift_right))
                link(nc.vector.tensor_copy(n_f[:], n_i[:]))
                link(nc.vector.tensor_tensor_scan(n_end[:], ones[0:1, 0:E], n_f[:], 0.0, ALU.mult, ALU.add))
                shape = [1, SLOTS, E]
                link(nc.vector.tensor_tensor(past[:], tile_no[:, :, None].to_broadcast(shape),
                                             n_end[:, None, :].to_broadcast(shape), ALU.is_ge))
                link(nc.vector.tensor_tensor(past_n[:], past[:], n_f[:, None, :].to_broadcast(shape), ALU.mult),
                     nc.vector.tensor_reduce(t_exp[:], past[:], AX_X, ALU.add))
                link(nc.vector.tensor_reduce(t_start[:], past_n[:], AX_X, ALU.add),
                     nc.vector.scalar_tensor_tensor(out=t_row[:], in0=t_exp[:], scalar=float(T // P), in1=tile_no,
                                                    op0=ALU.mult, op1=ALU.add))
                link(nc.vector.tensor_tensor(t_row[:], t_row[:], t_start[:], ALU.subtract),
                     nc.vector.tensor_scalar(tile_w[:], t_exp[:], float(E - 1), float(2 * EX_W), ALU.min, ALU.mult))
                nc.vector.tensor_scalar(tile_row[:], t_row[:], float(P), None, ALU.mult).then_inc(tiles_ready, 1)

            def gated(g, m):
                dve.wait_ge(silu_ready, SM * g + m + 1)
                nc.vector.scalar_tensor_tensor(out=hm[:], in0=UP, scalar=1 / WS, in1=silu[:], op0=ALU.mult,
                                               op1=ALU.mult).then_inc(hm_done, 1)
                dve.wait_ge(hh_ready, SM * g + m + 1)
                one = "p o t -> p (o t)"
                nc.vector.tensor_tensor(hTl[:, bass.ds(m, 1), :].rearrange(one), hm[:],
                                        hTh[:, bass.ds(m, 1), :].rearrange(one), ALU.subtract).then_inc(hl_ready, 1)

            def add_shared(g, q):
                dve.wait_ge(down_ready, Q * g + q + 1)
                r = x_tok[g % 3][:, q, :]
                nc.vector.scalar_tensor_tensor(out=r, in0=bank[4 + q % 2], scalar=1 / WS, in1=r, op0=ALU.mult,
                                               op1=ALU.add).then_inc(base_ready, 1)

            def mixed(g):
                for q in range(Q):
                    dve.wait_ge(outT_ready, Q * g + q + 1)
                    r = x_tok[g % 3][:, q, :]
                    nc.vector.scalar_tensor_tensor(out=r, in0=turn_bank("out", g, q), scalar=1 / WS, in1=r,
                                                   op0=ALU.mult, op1=ALU.add).then_inc(x1_done, 1)
                dve.wait_ge(x1_done, Q * (g + 1))
                moments(x_tok[g % 3], 2 * g + 2 if g < G - 1 else 2 * G - 1)
                normalise(x_tok[g % 3], xf_ready)

            def piece(dst, high, par, n, width):
                dve.wait_ge(piece_h, n + 1)
                nc.vector.scalar_tensor_tensor(out=dst, in0=stage[par][:, 0:width], scalar=WS, in1=high, op0=ALU.mult,
                                               op1=ALU.subtract).then_inc(piece_l, 1)

            def expert(e):
                for c in range(EX_PARTS):
                    at = e * (2 * EX_W) + c * EX_PIECE
                    piece(experts[:, bass.ds(at + EX_W, EX_PIECE)], experts[:, bass.ds(at, EX_PIECE)],
                          (SH_PIECES + c) % 2, SH_PIECES + e * EX_PARTS + c, EX_PIECE)

            dve.wait_ge(const_in, 48)
            nc.vector.tensor_copy(next_row[:], first_row).then_inc(hm_done, 1)
            values(0)
            dve.wait_ge(gate_split_h, 1)
            nc.vector.scalar_tensor_tensor(out=gate_l[:], in0=gate_raw[:], scalar=WS, in1=gate_h[:], op0=ALU.mult,
                                           op1=ALU.subtract).then_inc(gate_split_l, 1)
            skip_product(0, 0)
            for q in range(Q):
                skip_term(0, q)
            low_parts(0, 0)
            for g in range(G):
                s0 = g * HG
                low_parts(s0 + 1, 1)
                finish(s0, 0, g)
                if g == 0:
                    for i in range(3):
                        c = slice(i * SH_PIECE, (i + 1) * SH_PIECE)
                        piece(d_l[:, c], d_h[:, c], i % 2, i, SH_PIECE)
                else:
                    normed_low(g - 1)
                    pick(g - 1)
                if g < G - 1:
                    values(g + 1)
                with dve.Fori(0, 3) as j:
                    for u in range(2):
                        h = 1 + 2 * j + u
                        low_parts(s0 + h + 1, u)
                        finish(s0 + h, h, g)
                        if g == 0:
                            c = bass.ds((2 * j + u) * SH_PIECE, SH_PIECE)
                            piece(gu_l[:, c], gu_h[:, c], (1 + u) % 2, 3 + 2 * j + u, SH_PIECE)
                        else:
                            gated(g - 1, 2 * j + u)
                if g > 0:
                    pairs(g - 1)
                if g < G - 1:
                    skip_product(g + 1, 0)
                for q in range(Q):
                    if g < G - 1:
                        skip_term(g + 1, q)
                    if g > 0:
                        add_shared(g - 1, q)
                finish(s0 + HG - 1, HG - 1, g)
                if g < G - 1:
                    low_parts(s0 + HG, 0)
                mixed(g)
            normed_low(G - 1)
            pick(G - 1)
            with dve.Fori(0, early_experts) as m:
                gated(G - 1, m)
                expert(m)
            for m in range(early_experts, SM):
                gated(G - 1, m)
            pairs(G - 1)
            tile_table()
            for e in range(early_experts, E):
                expert(e)
                if e < E - 1:
                    add_shared(G - 1, 2 * (e - early_experts))
                    add_shared(G - 1, 2 * (e - early_experts) + 1)

            def tile_low(t, par):
                dve.wait_ge(r_xh, t + 1)
                nc.vector.tensor_tensor(xgl[par], bank[2], xgh[par], ALU.subtract).then_inc(r_xl, 1)

            def tile_gated(t):
                dve.wait_ge(r_silu, t + 1)
                nc.vector.scalar_tensor_tensor(out=hm[:, 0:FF], in0=bank[1][:, 0:FF], scalar=1 / WS,
                                               in1=silu[:, 0:FF], op0=ALU.mult, op1=ALU.mult).then_inc(r_hm, 1)

            def tile_hidden_low(t):
                dve.wait_ge(r_hh, t + 1)
                nc.vector.tensor_tensor(hgl, bank[3][:, 0:FK * P], hgh, ALU.subtract).then_inc(r_hl, 1)

            tile_low(0, 0)
            tile_gated(0)
            tile_low(1, 1)
            tile_hidden_low(0)
            with dve.Fori(0, (TILES - 3) // 2) as j:
                for u in range(1, 3):
                    t = 2 * j + u
                    tile_gated(t)
                    tile_low(t + 1, (u + 1) % 2)
                    tile_hidden_low(t)
            for t in range(TILES - 2, TILES):
                tile_gated(t)
                if t + 1 < TILES:
                    tile_low(t + 1, (t + 1) % 2)
                tile_hidden_low(t)


def constants():
    import numpy as np

    con = np.zeros((P, CONST_W), np.float32)
    p = np.arange(P)
    con[:, 0:P] = np.eye(P)
    con[:, P:2 * P] = p[:, None] // NH == p[None, :] // NH
    con[:, 2 * P:3 * P] = p[:, None] < p[None, :]
    con[:, 3 * P:4 * P] = 1
    c = 4 * P
    con[:, c:c + 8] = np.arange(8)
    con[:, c + 8:c + 12] = -0.5
    con[:, c + 12:c + 20] = np.arange(E) * T
    con[:, c + 20:c + 20 + SLOTS] = np.arange(SLOTS)
    con[:, c + 20 + SLOTS:] = (np.arange(Q)[None] * 2 + p[:, None] // RG) * S + p[:, None] % RG
    table = np.zeros((TROWS, 2), np.int32)
    table[:, 0] = T + np.arange(TROWS) % P
    return con, table, np.zeros((P, L), np.float32)


def kernel(x, fside_S2_0, ctx_2048, L0_xattn_k, L0_ffn_gate_w, L0_ffn_shared_wg, L0_ffn_shared_wu, L0_ffn_shared_wd,
           L0_ffn_exp_wg, L0_ffn_exp_wu, L0_ffn_exp_wd):
    import numpy as np
    import concourse.bacc as bacc
    from concourse.bass_utils import run_bass_kernel_spmd

    def rows(w, n):
        w = w.reshape(*w.shape[:-2], n, P, w.shape[-1])
        w = np.moveaxis(w, -3, -2)
        return w.reshape(*w.shape[:-2], n * w.shape[-1])

    def padded(w, n):
        return np.concatenate([w, np.zeros((*w.shape[:-1], n - w.shape[-1]), w.dtype)], -1)

    a = {k: np.asarray(v) for k, v in dict(
        x=x, skip=fside_S2_0, ctx=ctx_2048, k=L0_xattn_k, gate=L0_ffn_gate_w, sg=L0_ffn_shared_wg, su=L0_ffn_shared_wu,
        sd=L0_ffn_shared_wd, eg=L0_ffn_exp_wg, eu=L0_ffn_exp_wu, ed=L0_ffn_exp_wd).items()}
    con, table, zeros = constants()
    gu = np.concatenate([padded(a["sg"].T, SFP), padded(a["su"].T, SFP)], -1)
    sd = padded(a["sd"], SFP).T
    ed = a["ed"]
    whole = (FK - 1) * P
    last = np.concatenate([np.zeros((E, L, FK * P - FF), ed.dtype), ed[:, :, whole:]], -1)
    ed = np.concatenate([ed[:, :, 0:whole], last], -1)
    t = lambda w: np.swapaxes(w, -1, -2)
    arrays = {
        "x": a["x"], "ctx": a["ctx"], "skip": np.tile(a["skip"].reshape(G, RG).T, (2, 1)),
        "krev": padded(a["k"][:, ::-1], KREV),
        "gate_w": rows(a["gate"].T, LB),
        "shared_w": np.concatenate([rows(sd, SM), rows(gu, LB)], -1),
        "expert_w": np.concatenate([rows(t(a["eg"]), LB), rows(t(a["eu"]), LB), rows(t(ed), FK)], -1),
        "consts": con, "table0": table, "zeros": zeros,
    }
    arrays = {f"in_{k}": np.ascontiguousarray(v) for k, v in arrays.items()}
    nc = bacc.Bacc("TRN2", target_bir_lowering=False, num_devices=1)
    args = [nc.dram_tensor(k, v.shape, mybir.dt.from_np(v.dtype), kind="ExternalInput").ap() for k, v in arrays.items()]
    out = nc.dram_tensor("out", (T + P, L), F32, kind="ExternalOutput").ap()
    xattn_moe(nc, *args, out)
    r = run_bass_kernel_spmd(nc, [arrays], core_ids=[0])
    return r.results[0]["out"][0:T].reshape(B, S, L)
```

```python
from contextlib import ExitStack

import concourse.bass as bass
from concourse import mybir

ALU = mybir.AluOpType
ACT = mybir.ActivationFunctionType
AX_X = mybir.AxisListType.X
F32 = mybir.dt.float32
F16 = mybir.dt.float16
I32 = mybir.dt.int32
U32 = mybir.dt.uint32

P = 128
B, S, L = 8, 256, 512
NH = 8
H = S // NH
LB = L // P
HG = 8
G = H // HG
RG = HG * NH
TG = B * RG
Q = TG // P
T = B * S
COLS = B * NH * NH
E = 8
FF = 352
FK = -(-FF // P)
SFF = 704
SM = -(-SFF // P)
SFP = SM * P
SH_GU = LB * 2 * SFP
SH_W = SH_GU + SM * L
SH_PIECE = 1024
SH_PIECES = SH_W // SH_PIECE
EX_W = 2 * LB * FF + FK * L
EX_PARTS = 4
EX_PIECE = EX_W // EX_PARTS
TILES = 2 * T // P + E - 1
EROWS = T + P
TROWS = E * EROWS + P
RING = 4
EPS = 1e-5
ROUTE_SCALE = 2.5
WS = 256.0
SLOTS = -(-TILES // RING) * RING
CONST_W = 4 * P + 20 + SLOTS + Q
KREV = L + P


def xattn_moe(nc, x, ctx, ctx_hidden, skip, krev, gate_w, shared_w, expert_w, consts, table0, zeros, out):
    scaled = nc.dram_tensor("scaled_filters", [H, KREV], F32).ap()
    filters = bass.AP(scaled.tensor, 0, [[KREV, H], [1, P], [1, L]])
    x_rows = x.rearrange("b (g r) l -> g b r l", r=RG)
    ctx_rows = ctx.rearrange("b (g r) l -> g b r l", r=RG)
    out_rows = out[0:T, :].rearrange("(b g r) l -> g b r l", b=B, g=G)
    pair_rows = nc.dram_tensor("pair_rows", [TROWS, L], F32).ap()
    table = nc.dram_tensor("pair_table", [TROWS, 2], I32).ap()

    with ExitStack() as stack:
        def sb(name, shape, dt):
            return stack.enter_context(nc.sbuf_tensor(name, shape, dt))

        def sem(name):
            return stack.enter_context(nc.semaphore(name))

        ps = stack.enter_context(nc.psum_tensor("banks", [P, 8, 512], F32))

        arena = sb("arena", [P, E * EX_W], F32)
        place = [0]

        def carve(words):
            place[0] += words
            return arena[:, place[0] - words:place[0]]

        kv = [carve(LB * COLS) for _ in range(2)]
        kvh = [carve(LB * COLS // 2).bitcast(F16) for _ in range(2)]
        kvl = [carve(LB * COLS // 2).bitcast(F16) for _ in range(2)]
        prod = carve(LB * COLS)
        vT = [carve(LB * TG) for _ in range(2)]
        cT = [carve(LB * TG) for _ in range(2)]
        filt_raw = [carve(L) for _ in range(2)]
        fh = [carve(L // 2).bitcast(F16) for _ in range(2)]
        fl = [carve(L // 2).bitcast(F16) for _ in range(2)]
        ctx_tok = carve(Q * L).rearrange("p (q l) -> p q l", q=Q)
        x_tok2 = carve(Q * L).rearrange("p (q l) -> p q l", q=Q)
        filt_all = prod[0:H, 0:KREV]
        place[0] = E * EX_W - SH_W
        shared_gu = carve(SH_GU)
        shared_d = carve(SH_W - SH_GU)
        early_experts = (E * EX_W - SH_W) // EX_W
        gu_h, gu_l = shared_gu[:, 0:SH_GU // 2].bitcast(F16), shared_gu[:, SH_GU // 2:SH_GU].bitcast(F16)
        d_n = SH_W - SH_GU
        d_h, d_l = shared_d[:, 0:d_n // 2].bitcast(F16), shared_d[:, d_n // 2:d_n].bitcast(F16)
        experts = arena[:, :].bitcast(F16)

        x_tok = [sb(f"x_tok{i}", [P, Q, L], F32) for i in range(2)] + [x_tok2]
        normed = sb("normed", [P, Q, L], F32)
        mixT = sb("mixT", [P, LB * TG], F32)
        xfh = sb("xfh", [P, LB, TG], F16)
        xfl = sb("xfl", [P, LB, TG], F16)
        silu = sb("silu", [P, 512], F32)
        hm = sb("hm", [P, 512], F32)
        skipped = hm
        hTh = sb("hTh", [P, SM, TG], F16)
        hTl = sb("hTl", [P, SM, TG], F16)
        stages = sb("stages", [P, 2 * EX_PIECE], F32)
        stage = [stages[:, 0:EX_PIECE], stages[:, EX_PIECE:2 * EX_PIECE],
                 x_tok[1].rearrange("p q l -> p (q l)")[:, 0:EX_PIECE], mixT[:, 0:EX_PIECE]]
        kept = [stages[:, 0:Q * L].rearrange("p (q l) -> p q l", q=Q)] * 2 + [ctx_tok, normed]
        con = sb("con", [P, CONST_W], F32)
        ident, block8, before, ones = (con[:, i * P:(i + 1) * P] for i in range(4))
        iota8 = con[:, 4 * P:4 * P + 8]
        minus_half = con[:, 4 * P + 8:4 * P + 12]
        first_row = con[:, 4 * P + 12:4 * P + 20]
        tile_no = con[0:1, 4 * P + 20:4 * P + 20 + SLOTS]
        row_base = con[:, 4 * P + 20 + SLOTS:CONST_W]
        tok_ids = sb("tok_ids", [P, Q], I32)
        skip_col = sb("skip_col", [P, G], F32)
        gate_raw = sb("gate_raw", [P, LB * E], F32)
        gate_h = sb("gate_h", [P, LB * E], F16)
        gate_l = sb("gate_l", [P, LB * E], F16)
        stats = sb("stats", [P, Q, 6], F32)
        meanvar = sb("meanvar", [P, Q, 2], F32)
        var_eps = sb("var_eps", [P, Q], F32)
        rstd = sb("rstd", [P, Q], F32)
        score = sb("score", [P, Q, E], F32)
        top = sb("top", [P, Q, E], F32)
        topi = sb("topi", [P, Q, E], U32)
        topf = sb("topf", [P, Q, 2], F32)
        onehot = sb("onehot", [P, Q, 2, E], F32)
        picked = sb("picked", [P, Q, E], F32)
        rank = sb("rank", [P, Q, E], F32)
        rankhot = sb("rankhot", [P, Q, 2, E], F32)
        rowf = sb("rowf", [P, Q, 2], F32)
        row = sb("row", [P, Q, 2], I32)
        pair = sb("pair", [P, Q, 2, 2], I32)
        wsum = sb("wsum", [P, Q], F32)
        winv = sb("winv", [P, Q], F32)
        wtop = sb("wtop", [P, Q, 2], F32)
        next_row = sb("next_row", [P, E], F32)
        n_i = sb("n_i", [1, E], I32)
        n_f = sb("n_f", [1, E], F32)
        n_end = sb("n_end", [1, E], F32)
        pad_row = sb("pad_row", [1, E], I32)
        past, past_n = (mixT[0:1, EX_PIECE + i * SLOTS * E:EX_PIECE + (i + 1) * SLOTS * E]
                        .rearrange("p (t e) -> p t e", e=E) for i in range(2))
        t_start = mixT[0:1, EX_PIECE + 2 * SLOTS * E:EX_PIECE + 2 * SLOTS * E + SLOTS]
        t_exp = sb("t_exp", [1, SLOTS], F32)
        t_row = sb("t_row", [1, SLOTS], F32)
        tile_row = sb("tile_row", [1, SLOTS], I32)
        tile_w = sb("tile_w", [1, SLOTS], I32)
        tile_need = sb("tile_need", [1, SLOTS], I32)
        ids = [sb(f"ids{i}", [P, 2], I32) for i in range(RING)]
        xg = [normed[:, i, :] for i in range(RING)]
        yg = [x_tok[0][:, i, :] for i in range(RING)]
        xgh = [xfh[:, i, :] for i in range(2)]
        xgl = [xfl[:, i, :] for i in range(2)]
        hgh = xfh[:, 2, 0:FK * P]
        hgl = xfl[:, 2, 0:FK * P]

        const_in = sem("const_in")
        small_in = sem("small_in")
        x_in = [sem(f"x_in{g}") for g in range(G)]
        ctx_in = [sem(f"ctx_in{g}") for g in range(G)]
        cT_in = [sem(f"cT_in{g}") for g in range(G)]
        filt_all_in = sem("filt_all_in")
        filt_scaled = sem("filt_scaled")
        filt_stored = sem("filt_stored")
        filt_in = [sem(f"filt_in{i}") for i in range(2)]
        stage_in = [sem(f"stage_in{i}") for i in range(RING)]
        init_done = sem("init_done")
        base_stored = sem("base_stored")
        rows_kept = sem("rows_kept")
        rows_sent = sem("rows_sent")
        pads_stored = sem("pads_stored")
        pairs_stored = sem("pairs_stored")
        ids_in = [sem(f"ids_in{i}") for i in range(RING)]
        rows_in = [sem(f"rows_in{i}") for i in range(RING)]
        added = sem("added")
        kv_ready = sem("kv_ready")
        fh_ready = sem("fh_ready")
        fl_ready = sem("fl_ready")
        kvh_ready = sem("kvh_ready")
        kvl_ready = sem("kvl_ready")
        conv_ready = sem("conv_ready")
        prod_done = sem("prod_done")
        mix_done = sem("mix_done")
        v_ready = sem("v_ready")
        skip_ready = sem("skip_ready")
        tokT_ready = sem("tokT_ready")
        tokT_done = sem("tokT_done")
        skipsum_ready = sem("skipsum_ready")
        skip_done = sem("skip_done")
        var_ready = sem("var_ready")
        rstd_ready = sem("rstd_ready")
        outT_ready = sem("outT_ready")
        x1_done = sem("x1_done")
        xf_ready = sem("xf_ready")
        xfT_ready = sem("xfT_ready")
        xfh_ready = sem("xfh_ready")
        xfl_ready = sem("xfl_ready")
        logit_ready = sem("logit_ready")
        score_ready = sem("score_ready")
        picked_ready = sem("picked_ready")
        rank_ready = sem("rank_ready")
        rank_used = sem("rank_used")
        pair_ready = sem("pair_ready")
        gu_ready = sem("gu_ready")
        silu_ready = sem("silu_ready")
        hm_done = sem("hm_done")
        hh_ready = sem("hh_ready")
        hl_ready = sem("hl_ready")
        down_ready = sem("down_ready")
        base_ready = sem("base_ready")
        piece_h = sem("piece_h")
        shared_l = sem("shared_l")
        piece_l = sem("piece_l")
        gate_split_h = sem("gate_split_h")
        gate_split_l = sem("gate_split_l")
        tiles_ready = sem("tiles_ready")
        dve_step = sem("dve_step")
        pool_passed = sem("pool_passed")
        r_gu = sem("r_gu")
        r_silu = sem("r_silu")
        r_hm = sem("r_hm")
        r_xT = sem("r_xT")
        r_xh = sem("r_xh")
        r_xl = sem("r_xl")
        r_hT = sem("r_hT")
        r_hh = sem("r_hh")
        r_hl = sem("r_hl")
        r_down = sem("r_down")
        r_y = sem("r_y")

        bank = [ps[:, i, :] for i in range(8)]
        GATE, UP = bank[4], bank[5]

        def turns_of(name, g):
            if name == "prep":
                for q in range(Q):
                    yield tokT_done, Q * g + q + 1
                for q in range(Q):
                    yield skip_done, Q * g + q + 1
            elif name == "out":
                for q in range(Q):
                    yield x1_done, Q * g + q + 1
            elif name == "xf":
                for q in range(Q):
                    yield xfl_ready, Q * g + q + 1
                yield score_ready, g + 1
            elif name == "rank":
                yield rank_used, g + 1

        turn_order = [("prep", 0)]
        for g in range(G):
            turn_order += [("out", g - 1), ("xf", g - 1), ("rank", g - 1)] if g > 0 else []
            turn_order += [("prep", g + 1)] if g < G - 1 else []
        turn_order += [("out", G - 1), ("xf", G - 1), ("rank", G - 1)]
        turn_read = [t for name, g in turn_order for t in turns_of(name, g)]

        def turn_bank(name, g, k):
            n = sum(len(list(turns_of(*w))) for w in turn_order[:turn_order.index((name, g))])
            return bank[6 + (n + k) % 2]

        def backwards(v):
            return bass.AP(v.tensor, v.offset + L - 1, [v.ap[0], [-1, L]])

        def heads(v):
            return v.rearrange("p (a r) -> p a r", r=RG)

        block = stack.enter_context(nc.Block())


        @block.sync
        def _(sp):
            def load_filter(s, par):
                sp.dma_start(filt_raw[par], filters[bass.ds(s, 1), :, :].rearrange("o p l -> (o p) l")
                             ).then_inc(filt_in[par], 16)

            def next_filter(s, par):
                sp.wait_ge(fl_ready, s - 1)
                load_filter(s, par)

            def load_rows(dst, src, done):
                for b2 in range(2):
                    sp.dma_start(dst[b2 * RG:(b2 + 1) * RG, :, :],
                                 src.rearrange("(q t) r l -> t r q l", t=2)[b2]).then_inc(done, 16)

            def load_hidden(g):
                sp.dma_start(cT[g % 2], ctx_hidden[g]).then_inc(cT_in[g], 16)

            def store(dst, src, done):
                for b2 in range(2):
                    sp.dma_start(dst.rearrange("(q t) r l -> t r q l", t=2)[b2],
                                 src[b2 * RG:(b2 + 1) * RG, :, :]).then_inc(done, 16)

            def load_shared(i, par):
                sp.dma_start(stage[par][:, 0:SH_PIECE], shared_w[:, bass.ds(i * SH_PIECE, SH_PIECE)]
                             ).then_inc(stage_in[par], 16)

            def next_shared(i, par):
                sp.wait_ge(shared_l, i - 1)
                load_shared(i, par)

            def load_piece(e, c):
                sp.dma_start(stage[c], expert_w[bass.ds(e, 1), :, c * EX_PIECE:(c + 1) * EX_PIECE]
                             .rearrange("e p n -> (e p) n")).then_inc(stage_in[c], 16)

            def load_expert(e):
                for c in range(EX_PARTS):
                    sp.wait_ge(piece_l, (e - 1) * EX_PARTS + c + 1)
                    load_piece(e, c)

            load_rows(x_tok[0], x_rows[0], x_in[0])
            sp.dma_start(con[:], consts).then_inc(const_in, 16)
            sp.dma_start(filt_all, krev).then_inc(filt_all_in, 16)
            load_hidden(0)
            sp.dma_start(skip_col[:], skip).then_inc(small_in, 16)
            sp.dma_start(gate_raw[:], gate_w).then_inc(small_in, 16)
            load_rows(ctx_tok, ctx_rows[0], ctx_in[0])
            sp.wait_ge(filt_scaled, 1)
            sp.dma_start(scaled, filt_all).then_inc(filt_stored, 16)
            sp.wait_ge(filt_stored, 16)
            load_filter(0, 0)
            load_filter(1, 1)
            sp.wait_ge(ctx_in[0], 32)
            load_rows(x_tok[1], x_rows[1], x_in[1])
            load_shared(0, 0)
            load_shared(1, 1)
            sp.dma_start(table, table0).then_inc(init_done, 16)
            sp.dma_start(pair_rows[E * EROWS:TROWS, :], zeros).then_inc(init_done, 16)
            sp.dma_start(out[T:T + P, :], zeros).then_inc(init_done, 16)
            for g in range(G):
                s0 = g * HG
                next_filter(s0 + 2, 0)
                next_filter(s0 + 3, 1)
                if g == 0:
                    next_shared(2, 0)
                if g < G - 1:
                    if g > 0:
                        if g >= 2:
                            sp.wait_ge(base_stored, 32 * (g - 1))
                        load_rows(x_tok[(g + 1) % 3], x_rows[g + 1], x_in[g + 1])
                    sp.wait_ge(skip_done, Q * (g + 1))
                    load_rows(ctx_tok, ctx_rows[g + 1], ctx_in[g + 1])
                    if g > 0:
                        sp.wait_ge(mix_done, HG * g)
                    load_hidden(g + 1)
                if g > 0:
                    if g == 1:
                        sp.wait_ge(shared_l, SH_PIECES)
                    elif g == 2:
                        sp.wait_ge(rows_sent, 16 * 2 * Q)
                    sp.wait_ge(xf_ready, Q * g)
                    sp.dma_start(kept[g - 1], normed[:]).then_inc(rows_kept, 16)
                with sp.Fori(0, 3 if g < G - 1 else 2) as j:
                    for u in range(2):
                        next_filter(s0 + 4 + 2 * j + u, u)
                        if g == 0:
                            next_shared(3 + 2 * j + u, (1 + u) % 2)
                if 0 < g < G - 1:
                    sp.wait_ge(base_ready, Q * g)
                    store(out_rows[g - 1], x_tok[(g - 1) % 3], base_stored)
            sp.wait_ge(rows_sent, 16 * 2 * Q * 2)
            load_piece(0, 0)
            load_piece(0, 1)
            sp.wait_ge(base_stored, 32 * 2)
            load_piece(0, 2)
            sp.wait_ge(outT_ready, Q * G)
            load_piece(0, 3)
            with sp.Fori(1, 4) as e:
                load_expert(e)
            sp.wait_ge(base_ready, Q * (G - 1))
            store(out_rows[G - 2], x_tok[(G - 2) % 3], base_stored)
            sp.wait_ge(tiles_ready, 1)
            for e in range(E):
                r = sp.value_load(pad_row[0:1, e:e + 1], min_val=e * EROWS, max_val=e * EROWS + T)
                sp.dma_start(pair_rows[bass.ds(r, P), :], zeros).then_inc(pads_stored, 16)
            with sp.Fori(4, E) as e:
                load_expert(e)

            def load_tile(t, slot):
                r = sp.value_load(tile_row[0:1, bass.ds(t, 1)], min_val=0, max_val=TROWS - P)
                sp.dma_start(xg[slot], pair_rows[bass.ds(r, P), :]).then_inc(rows_in[slot], 16)
                sp.dma_start(ids[slot][:], table[bass.ds(r, P), :]).then_inc(ids_in[slot], 16)

            sp.wait_ge(pads_stored, 16 * E)
            sp.wait_ge(rows_sent, 16 * 2 * Q * G)
            sp.wait_ge(pairs_stored, 16 * 2 * Q * G)
            for t in range(RING):
                load_tile(t, t)
            sp.wait_ge(base_ready, Q * G)
            store(out_rows[G - 1], x_tok[(G - 1) % 3], base_stored)
            with sp.Fori(0, TILES // RING - 1) as j:
                for u in range(RING):
                    sp.wait_ge(added, 16 * (j * RING + u + 1))
                    load_tile(RING + j * RING + u, u)
            for t in range(TILES // RING * RING, TILES):
                sp.wait_ge(added, 16 * (t - RING + 1))
                load_tile(t, t % RING)
            sp.wait_ge(base_stored, 32 * G)
            sp.wait_ge(init_done, 48)
            sp.wait_ge(added, 16 * TILES)

        @block.gpsimd
        def _(pool):
            def outer(s, h, g, par):
                v = heads(vT[g % 2])[:, :, bass.ds(h * NH, NH)]
                c = heads(cT[g % 2])[:, :, bass.ds(h * NH, NH)]
                shape = [P, LB * B, NH, NH]
                nc.gpsimd.tensor_tensor(kv[par].rearrange("p (a i j) -> p a i j", i=NH, j=NH),
                                        v[:, :, :, None].to_broadcast(shape), c[:, :, None, :].to_broadcast(shape),
                                        ALU.mult).then_inc(kv_ready, 1)

            def inverse_root(n):
                pool.wait_ge(var_ready, n + 1)
                nc.gpsimd.tensor_tensor(rstd[:], var_eps[:], minus_half, ALU.pow).then_inc(rstd_ready, 1)

            def send_pairs(g):
                pool.wait_ge(pair_ready, g + 1)
                if g < G - 1:
                    pool.wait_ge(rows_kept, 16 * (g + 1))
                for q in range(Q):
                    for k in range(2):
                        place = bass.IndirectOffsetOnAxis(ap=row[:, q, k:k + 1], axis=0)
                        nc.gpsimd.indirect_dma_start(out=pair_rows, out_offset=place, in_=kept[g][:, q, :],
                                                     in_offset=None).then_inc(rows_sent, 16)
                for q in range(Q):
                    for k in range(2):
                        place = bass.IndirectOffsetOnAxis(ap=row[:, q, k:k + 1], axis=0)
                        nc.gpsimd.indirect_dma_start(out=table, out_offset=place, in_=pair[:, q, k, :],
                                                     in_offset=None).then_inc(pairs_stored, 16)

            def filter_low(s, par):
                pool.wait_ge(fh_ready, s + 1)
                nc.gpsimd.tensor_tensor(fl[par], backwards(filt_raw[par]), fh[par], ALU.subtract).then_inc(fl_ready, 1)

            def piece(i, par):
                at = i * SH_PIECE
                down_pieces = d_n // SH_PIECE
                if isinstance(i, int) and i < down_pieces:
                    low, high = (w[:, at:at + SH_PIECE] for w in (d_l, d_h))
                else:
                    low, high = (w[:, bass.ds((i - down_pieces) * SH_PIECE, SH_PIECE)] for w in (gu_l, gu_h))
                pool.wait_ge(piece_h, i + 1)
                nc.gpsimd.tensor_tensor(low, stage[par][:, 0:SH_PIECE], high, ALU.subtract).then_inc(shared_l, 1)

            pool.wait_ge(const_in, 16)
            inverse_root(0)
            pool.wait_ge(tokT_done, Q)
            pool.wait_ge(cT_in[0], 16)
            outer(0, 0, 0, 0)
            filter_low(0, 0)
            outer(1, 1, 0, 1)
            filter_low(1, 1)
            piece(0, 0)
            for g in range(G):
                s0 = g * HG
                pool.wait_ge(kvl_ready, s0 + 1)
                outer(s0 + 2, 2, g, 0)
                if g > 0:
                    inverse_root(2 * g)
                filter_low(s0 + 2, 0)
                if g == 0:
                    piece(1, 1)
                pool.wait_ge(kvl_ready, s0 + 2)
                outer(s0 + 3, 3, g, 1)
                filter_low(s0 + 3, 1)
                if g == 0:
                    piece(2, 0)
                if g < G - 1:
                    inverse_root(2 * g + 1)
                with pool.Fori(0, 2) as j:
                    for u in range(2):
                        pool.wait_ge(kvl_ready, s0 + 3 + 2 * j + u)
                        outer(s0 + 4 + 2 * j + u, 4 + 2 * j + u, g, u)
                        if g == 0:
                            piece(3 + 2 * j + u, (1 + u) % 2)
                        filter_low(s0 + 4 + 2 * j + u, u)
                if g < G - 1:
                    pool.wait_ge(tokT_done, Q * (g + 2))
                    pool.wait_ge(cT_in[g + 1], 16)
                    for h in range(2):
                        pool.wait_ge(kvl_ready, s0 + HG + h - 1)
                        outer(s0 + HG + h, h, g + 1, h)
                        filter_low(s0 + HG + h, h)
                if g == 0:
                    piece(7, 1)
                    piece(8, 0)
                    pool.wait_ge(init_done, 48)
                else:
                    send_pairs(g - 1)
            inverse_root(2 * G - 1)
            send_pairs(G - 1)

            def add_tile(t, slot):
                pool.wait_ge(r_y, t + 1)
                if not isinstance(t, int) or t > 0:
                    pool.wait_ge(added, 16 * t)
                pool.sem_inc(pool_passed, 1)
                pool.wait_ge(base_stored, 32 * G)
                nc.gpsimd.indirect_dma_start(
                    out=out, out_offset=bass.IndirectOffsetOnAxis(ap=ids[slot][:, 0:1], axis=0),
                    in_=yg[slot], in_offset=None, compute_op=ALU.add).then_inc(added, 16)

            add_tile(0, 0)
            with pool.Fori(0, (TILES - 3) // RING) as j:
                for u in range(1, RING + 1):
                    add_tile(RING * j + u, u % RING)
            for t in range(TILES - 2, TILES):
                add_tile(t, t % RING)

        @block.tensor
        def _(pe):
            turn = [0]

            def take():
                k = turn[0]
                turn[0] += 1
                if k >= 2:
                    pe.wait_ge(*turn_read[k - 2])
                return bank[6 + k % 2]

            def split_products(dst, w, x, n):
                for k in range(n):
                    (wh, wl), (xh, xl) = w(k), x(k)
                    nc.tensor.matmul(dst, wh, xh, start=(k == 0), stop=False)
                    nc.tensor.matmul(dst, wh, xl, start=False, stop=False)
                    last = nc.tensor.matmul(dst, wl, xh, start=False, stop=(k == n - 1))
                return last

            def convolve(s, par, first=False):
                pe.wait_ge(kvl_ready, s + 1)
                pe.wait_ge(fl_ready, s + 1)
                for n in range(LB):
                    if not first:
                        pe.wait_ge(prod_done, LB * s - LB + 1 + n)
                    last = split_products(
                        bank[n],
                        lambda m: (fh[par][:, (n - m) * P:(n - m + 1) * P], fl[par][:, (n - m) * P:(n - m + 1) * P]),
                        lambda m: (kvh[par][:, m * COLS:(m + 1) * COLS], kvl[par][:, m * COLS:(m + 1) * COLS]), n + 1)
                    last.then_inc(conv_ready, 1)

            def transpose_tile(dst, src, done):
                for lb in range(LB):
                    last = nc.tensor.transpose(dst[:, lb * P:(lb + 1) * P], src(lb), ident)
                last.then_inc(done, 1)

            def prepare(g):
                for q in range(Q):
                    t = take()
                    pe.wait_ge(v_ready, Q * g + q + 1)
                    transpose_tile(t, lambda lb: normed[:, q, lb * P:(lb + 1) * P], tokT_ready)

            def skip_sum(g, q):
                t = take()
                pe.wait_ge(skip_ready, Q * g + q + 1)
                nc.tensor.matmul(t, block8, skipped[:], start=True, stop=True).then_inc(skipsum_ready, 1)

            def mix_out(g):
                pe.wait_ge(mix_done, HG * (g + 1))
                for q in range(Q):
                    transpose_tile(take(), lambda lb: mixT[:, lb * TG + q * P:lb * TG + (q + 1) * P], outT_ready)

            def normed_out(g, q):
                t = take()
                pe.wait_ge(xf_ready, Q * g + q + 1)
                transpose_tile(t, lambda lb: normed[:, q, lb * P:(lb + 1) * P], xfT_ready)

            def logits(g):
                t = take()
                pe.wait_ge(xfl_ready, Q * (g + 1))
                pe.wait_ge(gate_split_l, 1)
                for q in range(Q):
                    last = split_products(
                        t[:, q * E:(q + 1) * E],
                        lambda lb: (xfh[:, lb, q * P:(q + 1) * P], xfl[:, lb, q * P:(q + 1) * P]),
                        lambda lb: (gate_h[:, lb * E:(lb + 1) * E], gate_l[:, lb * E:(lb + 1) * E]), LB)
                last.then_inc(logit_ready, 1)

            def ranks(g):
                t = take()
                pe.wait_ge(picked_ready, g + 1)
                for q in range(Q + 1):
                    for k in range(q):
                        last = nc.tensor.matmul(t[:, q * E:(q + 1) * E], ones, picked[:, k, :],
                                                start=(k == 0), stop=(k == Q - 1))
                    if q < Q:
                        nc.tensor.matmul(t[:, q * E:(q + 1) * E], before, picked[:, q, :], start=(q == 0), stop=True)
                last.then_inc(rank_ready, 1)

            def gate_up(g, m, banks=(GATE, UP), ahead=0):
                pe.wait_ge(hm_done, SM * g + m + 1 - ahead)
                if g > 0:
                    pe.wait_ge(base_ready, Q * g)
                for half, dst in enumerate(banks):
                    last = split_products(
                        dst,
                        lambda lb: (gu_h[:, bass.ds((2 * lb + half) * SFP + m * P, P)],
                                    gu_l[:, bass.ds((2 * lb + half) * SFP + m * P, P)]),
                        lambda lb: (xfh[:, lb, :], xfl[:, lb, :]), LB)
                last.then_inc(gu_ready, 1)

            def down(g, q):
                if q == 0:
                    pe.wait_ge(hl_ready, SM * (g + 1))
                if q >= 2:
                    pe.wait_ge(base_ready, Q * g + q - 1)
                last = split_products(
                    bank[4 + q % 2],
                    lambda k: (hTh[:, k, q * P:(q + 1) * P], hTl[:, k, q * P:(q + 1) * P]),
                    lambda k: (d_h[:, k * L:(k + 1) * L], d_l[:, k * L:(k + 1) * L]), SM)
                last.then_inc(down_ready, 1)

            pe.wait_ge(const_in, 16)
            prepare(0)
            skip_sum(0, 0)
            skip_sum(0, 1)
            for g in range(G):
                s0 = g * HG
                convolve(s0, 0, first=(g == 0))
                if g > 0:
                    mix_out(g - 1)
                convolve(s0 + 1, 1)
                if g == 1:
                    pe.wait_ge(shared_l, SH_PIECES)
                if g > 0:
                    normed_out(g - 1, 0)
                    normed_out(g - 1, 1)
                else:
                    skip_sum(0, 2)
                convolve(s0 + 2, 0)
                if g > 0:
                    normed_out(g - 1, 2)
                    normed_out(g - 1, 3)
                    logits(g - 1)
                    gate_up(g - 1, 0)
                else:
                    skip_sum(0, 3)
                convolve(s0 + 3, 1)
                if g > 0:
                    gate_up(g - 1, 1)
                with pe.Fori(0, 2) as j:
                    for u in range(2):
                        convolve(s0 + 4 + 2 * j + u, u)
                        if g > 0:
                            gate_up(g - 1, 2 + 2 * j + u)
                if g > 0:
                    ranks(g - 1)
                if g < G - 1:
                    prepare(g + 1)
                    for q in range(Q):
                        skip_sum(g + 1, q)
                        if g > 0:
                            down(g - 1, q)
            down(G - 2, 0)
            down(G - 2, 1)
            mix_out(G - 1)
            down(G - 2, 2)
            down(G - 2, 3)
            for q in range(Q):
                normed_out(G - 1, q)
            logits(G - 1)
            def weights_of(t):
                return pe.value_load(tile_w[0:1, bass.ds(t, 1)], min_val=0, max_val=(E - 1) * 2 * EX_W)

            def need_of(t):
                return pe.value_load(tile_need[0:1, t:t + 1], min_val=EX_PARTS, max_val=E * EX_PARTS)

            pe.wait_ge(prod_done, LB * H)
            pairs_of_banks = ((GATE, UP), (bank[0], bank[1]))
            gate_up(G - 1, 0)
            ranks(G - 1)
            with pe.Fori(0, (SM - 2) // 2) as j:
                for u in range(2):
                    gate_up(G - 1, 1 + 2 * j + u, pairs_of_banks[(1 + u) % 2], 1)
            gate_up(G - 1, SM - 1, pairs_of_banks[(SM - 1) % 2], 1)
            pe.wait_ge(tiles_ready, 1)
            first_weights, first_need = weights_of(0), need_of(0)
            for q in range(Q):
                down(G - 1, q)

            def tile_in(t, slot, n):
                pe.wait_ge(rows_in[slot], 16 * n)
                transpose_tile(bank[2], lambda lb: xg[slot][:, lb * P:(lb + 1) * P], r_xT)

            def tile_gate_up(t, par, w):
                pe.wait_ge(r_xl, t + 1)
                for half in range(2):
                    last = split_products(
                        bank[half][:, 0:FF],
                        lambda lb: (xgh[par][:, lb * P:(lb + 1) * P], xgl[par][:, lb * P:(lb + 1) * P]),
                        lambda lb: (experts[:, bass.ds(w + (half * LB + lb) * FF, FF)],
                                    experts[:, bass.ds(w + EX_W + (half * LB + lb) * FF, FF)]), LB)
                last.then_inc(r_gu, 1)

            def tile_hidden(t):
                pe.wait_ge(r_hm, t + 1)
                for k in range(FK):
                    c = min(k * P, FF - P)
                    last = nc.tensor.transpose(bank[3][:, k * P:(k + 1) * P], hm[:, c:c + P], ident)
                last.then_inc(r_hT, 1)

            def tile_down(t, w):
                pe.wait_ge(r_hl, t + 1)
                if not isinstance(t, int) or t > 0:
                    pe.wait_ge(r_y, t)
                last = split_products(
                    bank[4],
                    lambda k: (hgh[:, k * P:(k + 1) * P], hgl[:, k * P:(k + 1) * P]),
                    lambda k: (experts[:, bass.ds(w + 2 * LB * FF + k * L, L)],
                               experts[:, bass.ds(w + EX_W + 2 * LB * FF + k * L, L)]), FK)
                last.then_inc(r_down, 1)

            tile_in(0, 0, 1)
            pe.wait_ge(piece_l, first_need)
            tile_gate_up(0, 0, first_weights)
            tile_in(1, 1, 1)
            tile_hidden(0)
            for t in range(1, RING + 1):
                w, need = weights_of(t), need_of(t)
                pe.wait_ge(piece_l, need)
                tile_gate_up(t, t % 2, w)
                tile_in(t + 1, (t + 1) % RING, (t + 1) // RING + 1)
                if t == 1:
                    pe.wait_ge(base_ready, Q * G)
                tile_down(t - 1, weights_of(t - 1))
                tile_hidden(t)
            pe.wait_ge(piece_l, E * EX_PARTS)
            with pe.Fori(1, (TILES - 3) // RING) as j:
                for u in range(1, RING + 1):
                    t = RING * j + u
                    tile_gate_up(t, u % 2, weights_of(t))
                    tile_in(t + 1, (u + 1) % RING, j + (u + 1) // RING + 1)
                    tile_down(t - 1, weights_of(t - 1))
                    tile_hidden(t)
            for t in range(TILES - 2, TILES):
                tile_gate_up(t, t % 2, weights_of(t))
                if t + 1 < TILES:
                    tile_in(t + 1, (t + 1) % RING, (t + 1) // RING + 1)
                tile_down(t - 1, weights_of(t - 1))
                tile_hidden(t)
            tile_down(TILES - 1, weights_of(TILES - 1))

        @block.scalar
        def _(act):
            def high_parts(s, par, n, reuse=True):
                act.wait_ge(filt_in[par], 16 * n)
                if reuse:
                    act.wait_ge(conv_ready, LB * s - LB)
                nc.scalar.activation(fh[par], backwards(filt_raw[par]), ACT.Copy).then_inc(fh_ready, 1)
                act.wait_ge(kv_ready, s + 1)
                nc.scalar.activation(kvh[par], kv[par], ACT.Copy).then_inc(kvh_ready, 1)

            def turned(g):
                if g >= 2:
                    act.wait_ge(mix_done, HG * (g - 1))
                for q in range(Q):
                    act.wait_ge(tokT_ready, Q * g + q + 1)
                    nc.scalar.copy(vT[g % 2].rearrange("p (a t) -> p a t", a=LB)[:, :, q * P:(q + 1) * P],
                                   turn_bank("prep", g, q).rearrange("p (a t) -> p a t", a=LB)
                                   ).then_inc(tokT_done, 1)

            def normed_high(g):
                if g > 0:
                    act.wait_ge(gu_ready, SM * g)
                for q in range(Q):
                    act.wait_ge(xfT_ready, Q * g + q + 1)
                    nc.scalar.copy(xfh[:, :, q * P:(q + 1) * P],
                                   turn_bank("xf", g, q).rearrange("p (a t) -> p a t", a=LB)).then_inc(xfh_ready, 1)

            def scores(g):
                act.wait_ge(logit_ready, g + 1)
                nc.scalar.activation(score[:], turn_bank("xf", g, Q)[:, 0:Q * E].rearrange("p (q e) -> p q e", e=E),
                                     ACT.Sigmoid, scale=1 / WS).then_inc(score_ready, 1)

            def gated(g, m, gate=GATE):
                act.wait_ge(gu_ready, SM * g + m + 1)
                nc.scalar.activation(silu[:], gate, ACT.Silu, scale=1 / WS).then_inc(silu_ready, 1)
                act.wait_ge(hm_done, SM * g + m + 2)
                if g > 0:
                    act.wait_ge(down_ready, Q * g)
                nc.scalar.copy(hTh[:, bass.ds(m, 1), :].rearrange("p o t -> p (o t)"), hm[:]).then_inc(hh_ready, 1)

            def piece(dst, par, n, width, scaled_too=False):
                act.wait_ge(stage_in[par], 16 * n)
                raw = stage[par][:, 0:width]
                high = nc.scalar.activation(dst, raw, ACT.Copy, scale=WS)
                if scaled_too:
                    high = nc.scalar.activation(raw, raw, ACT.Copy, scale=WS)
                high.then_inc(piece_h, 1)

            def expert(e, parts=range(EX_PARTS)):
                for c in parts:
                    shared = len(range(c, SH_PIECES, 2)) if c < 2 else 0
                    piece(experts[:, bass.ds(e * (2 * EX_W) + c * EX_PIECE, EX_PIECE)], c, shared + e + 1, EX_PIECE)

            def shared(i, par, n):
                down_pieces = d_n // SH_PIECE
                if isinstance(i, int) and i < down_pieces:
                    piece(d_h[:, i * SH_PIECE:(i + 1) * SH_PIECE], par, n, SH_PIECE, True)
                else:
                    piece(gu_h[:, bass.ds((i - down_pieces) * SH_PIECE, SH_PIECE)], par, n, SH_PIECE, True)

            act.wait_ge(filt_all_in, 16)
            nc.scalar.activation(filt_all, filt_all, ACT.Copy, scale=WS).then_inc(filt_scaled, 1)
            act.wait_ge(small_in, 32)
            nc.scalar.activation(gate_h[:], gate_raw[:], ACT.Copy, scale=WS).then_inc(gate_split_h, 1)
            turned(0)
            high_parts(0, 0, 1, reuse=False)
            for g in range(G):
                s0 = g * HG
                high_parts(s0 + 1, 1, s0 // 2 + 1, reuse=(g > 0))
                if g == 0:
                    shared(0, 0, 1)
                high_parts(s0 + 2, 0, s0 // 2 + 2)
                if g == 0:
                    shared(1, 1, 1)
                else:
                    normed_high(g - 1)
                    scores(g - 1)
                high_parts(s0 + 3, 1, s0 // 2 + 2)
                if g == 0:
                    shared(2, 0, 2)
                else:
                    gated(g - 1, 0)
                with act.Fori(0, 2) as j:
                    for u in range(2):
                        if g == 0:
                            shared(3 + 2 * j + u, (1 + u) % 2, j + 2 + u)
                        high_parts(s0 + 4 + 2 * j + u, u, s0 // 2 + 3 + j)
                        if g > 0:
                            gated(g - 1, 1 + 2 * j + u)
                if g > 0:
                    gated(g - 1, SM - 1)
                if g < G - 1:
                    turned(g + 1)
                    high_parts(s0 + HG, 0, s0 // 2 + HG // 2 + 1)
                if g == 0:
                    shared(7, 1, 4)
                    shared(8, 0, 5)
            act.wait_ge(mix_done, H)
            expert(0)
            normed_high(G - 1)
            expert(1)
            scores(G - 1)
            gates = (GATE, bank[0])
            expert(2)
            gated(G - 1, 0)
            act.wait_ge(rows_sent, 16 * 2 * Q * (G - 1))
            with act.Fori(0, (SM - 2) // 2) as j:
                for u in range(2):
                    gated(G - 1, 1 + 2 * j + u, gates[(1 + u) % 2])
                    expert(3 + j, range(2 * u, 2 * u + 2))
            gated(G - 1, SM - 1, gates[(SM - 1) % 2])
            act.wait_ge(base_stored, 32 * (G - 1))
            for e in range(early_experts, E):
                if e == E - 1:
                    act.wait_ge(down_ready, Q * G)
                expert(e)

            def tile_high(t, par):
                act.wait_ge(r_xT, t + 1)
                nc.scalar.copy(xgh[par], bank[2]).then_inc(r_xh, 1)

            def tile_silu(t):
                act.wait_ge(r_gu, t + 1)
                nc.scalar.activation(silu[:, 0:FF], bank[0][:, 0:FF], ACT.Silu, scale=1 / WS).then_inc(r_silu, 1)

            def tile_out(t, slot, n):
                act.wait_ge(ids_in[slot], 16 * n)
                act.wait_ge(r_down, t + 1)
                if not isinstance(t, int) or t >= RING:
                    act.wait_ge(added, 16 * (t - RING + 1))
                nc.scalar.activation(yg[slot], bank[4], ACT.Copy, scale=ids[slot][:, 1:2].bitcast(F32)
                                     ).then_inc(r_y, 1)

            def tile_hidden_high(t):
                act.wait_ge(r_hT, t + 1)
                nc.scalar.copy(hgh, bank[3][:, 0:FK * P]).then_inc(r_hh, 1)

            tile_high(0, 0)
            tile_silu(0)
            tile_high(1, 1)
            tile_hidden_high(0)
            for t in range(1, RING + 1):
                tile_silu(t)
                tile_high(t + 1, (t + 1) % 2)
                if t == 1:
                    act.wait_ge(base_stored, 32 * G)
                tile_out(t - 1, (t - 1) % RING, (t - 1) // RING + 1)
                tile_hidden_high(t)
            with act.Fori(1, (TILES - 3) // RING) as j:
                for u in range(1, RING + 1):
                    t = RING * j + u
                    tile_silu(t)
                    tile_high(t + 1, (u + 1) % 2)
                    tile_out(t - 1, u - 1, j + 1)
                    tile_hidden_high(t)
            for t in range(TILES - 2, TILES):
                tile_silu(t)
                if t + 1 < TILES:
                    tile_high(t + 1, (t + 1) % 2)
                tile_out(t - 1, (t - 1) % RING, (t - 1) // RING + 1)
                tile_hidden_high(t)
            tile_out(TILES - 1, (TILES - 1) % RING, (TILES - 1) // RING + 1)

        @block.vector
        def _(dve):
            steps = [0]

            def link(*ins):
                for i in ins:
                    i.then_inc(dve_step, 1)
                    steps[0] += 1
                dve.wait_ge(dve_step, steps[0])

            def low_parts(s, par):
                dve.wait_ge(kvh_ready, s + 1)
                nc.vector.tensor_tensor(kvl[par], kv[par], kvh[par], ALU.subtract).then_inc(kvl_ready, 1)

            def finish(s, h, g):
                products(s, h, g)
                total(s, h)

            def products(s, h, g):
                if not isinstance(s, int) or s > 0:
                    dve.wait_ge(mix_done, s)
                for n in range(LB):
                    dve.wait_ge(conv_ready, LB * s + n + 1)
                    c = heads(cT[g % 2])[:, n * B:(n + 1) * B, bass.ds(h * NH, NH)]
                    nc.vector.tensor_tensor(
                        prod[:, n * COLS:(n + 1) * COLS].rearrange("p (b i j) -> p b i j", i=NH, j=NH),
                        bank[n].rearrange("p (b i j) -> p b i j", i=NH, j=NH),
                        c[:, :, :, None].to_broadcast([P, B, NH, NH]), ALU.mult).then_inc(prod_done, 1)

            def total(s, h):
                dve.wait_ge(prod_done, LB * s + LB)
                nc.vector.tensor_reduce(heads(mixT)[:, :, bass.ds(h * NH, NH)],
                                        prod.rearrange("p (a i j) -> p a j i", i=NH, j=NH), AX_X, ALU.add
                                        ).then_inc(mix_done, 1)

            def moments(src):
                link(*[nc.vector.bn_stats(stats[:, q, :], src[:, q, :]) for q in range(Q)])
                link(*[nc.vector.bn_aggr(meanvar[:, q, :], stats[:, q, :]) for q in range(Q)])
                nc.vector.tensor_scalar(var_eps[:], meanvar[:, :, 1], EPS, None, ALU.add).then_inc(var_ready, 1)

            def normalise(src, n, done):
                dve.wait_ge(rstd_ready, n + 1)
                for q in range(Q):
                    nc.vector.tensor_scalar(normed[:, q, :], src[:, q, :], meanvar[:, q, 0:1], rstd[:, q:q + 1],
                                            ALU.subtract, ALU.mult).then_inc(done, 1)

            def value_moments(g):
                dve.wait_ge(x_in[g], 32)
                moments(x_tok[g % 3])

            def values(g):
                if g >= 2:
                    dve.wait_ge(rows_kept, 16 * (g - 1))
                    dve.wait_ge(xfT_ready, Q * (g - 1))
                normalise(x_tok[g % 3], 0 if g == 0 else 2 * g - 1, v_ready)

            def skip_product(g, q):
                if q > 0:
                    dve.wait_ge(skipsum_ready, Q * g + q)
                dve.wait_ge(v_ready, Q * g + q + 1)
                dve.wait_ge(ctx_in[g], 32)
                nc.vector.scalar_tensor_tensor(out=skipped[:], in0=ctx_tok[:, q, :], scalar=skip_col[:, g:g + 1],
                                               in1=normed[:, q, :], op0=ALU.mult, op1=ALU.mult).then_inc(skip_ready, 1)

            def skip_term(g, q):
                dve.wait_ge(skipsum_ready, Q * g + q + 1)
                if q + 1 < Q:
                    skip_product(g, q + 1)
                c, r = ctx_tok[:, q, :], x_tok[g % 3][:, q, :]
                t = nc.vector.tensor_tensor(c, turn_bank("prep", g, 2 * Q + q), c, ALU.mult)
                link(t)
                nc.vector.tensor_tensor(r, r, c, ALU.add).then_inc(skip_done, 1)

            def normed_low(g, tiles=range(Q)):
                for q in tiles:
                    dve.wait_ge(xfh_ready, Q * g + q + 1)
                    c = slice(q * P, (q + 1) * P)
                    nc.vector.tensor_tensor(xfl[:, :, c], turn_bank("xf", g, q).rearrange("p (a t) -> p a t", a=LB),
                                            xfh[:, :, c], ALU.subtract).then_inc(xfl_ready, 1)

            def pick(g):
                dve.wait_ge(score_ready, g + 1)
                link(*[nc.vector.max(top[:, q, :], score[:, q, :]) for q in range(Q)])
                link(*[nc.vector.max_index(topi[:, q, :], top[:, q, :], score[:, q, :]) for q in range(Q)])
                link(nc.vector.tensor_copy(topf[:], topi[:, :, 0:2]))
                shape = [P, Q, 2, E]
                for k in range(2):
                    shape = [P, Q, E]
                    i = nc.vector.tensor_tensor(onehot[:, :, k, :], iota8[:, None, :].to_broadcast(shape),
                                                topf[:, :, k:k + 1].to_broadcast(shape), ALU.is_equal)
                    link(i)
                nc.vector.tensor_tensor(picked[:], onehot[:, :, 0, :], onehot[:, :, 1, :], ALU.add
                                        ).then_inc(picked_ready, 1)

            def pairs(g):
                t = turn_bank("rank", g, 0)
                if g > 0:
                    dve.wait_ge(pairs_stored, 16 * 2 * Q * g)
                    dve.wait_ge(rows_sent, 16 * 2 * Q * g)
                dve.wait_ge(rank_ready, g + 1)
                link(nc.vector.tensor_tensor(rank[:], t[:, 0:Q * E].rearrange("p (q e) -> p q e", e=E),
                                             next_row[:, None, :].to_broadcast([P, Q, E]), ALU.add))
                nc.vector.tensor_tensor(next_row[:], next_row[:], t[:, Q * E:(Q + 1) * E], ALU.add
                                        ).then_inc(rank_used, 1)
                for k in range(2):
                    i = nc.vector.tensor_tensor(rankhot[:, :, k, :], onehot[:, :, k, :], rank[:], ALU.mult)
                    link(i)
                link(nc.vector.tensor_reduce(rowf[:], rankhot[:], AX_X, ALU.add))
                link(nc.vector.tensor_copy(row[:], rowf[:]),
                     nc.vector.tensor_scalar(tok_ids[:], row_base, float(RG * g), None, ALU.add),
                     nc.vector.tensor_tensor(wsum[:], top[:, :, 0], top[:, :, 1], ALU.add))
                link(nc.vector.tensor_scalar(wsum[:], wsum[:], 1e-20, None, ALU.add))
                link(nc.vector.reciprocal(winv[:], wsum[:]))
                link(nc.vector.tensor_tensor(wtop[:], top[:, :, 0:2], winv[:, :, None].to_broadcast([P, Q, 2]), ALU.mult))
                link(nc.vector.tensor_scalar(pair[:, :, :, 1].bitcast(F32), wtop[:], ROUTE_SCALE / WS, None, ALU.mult),
                     nc.vector.tensor_copy(pair[:, :, 0, 0], tok_ids[:]))
                nc.vector.tensor_copy(pair[:, :, 1, 0], tok_ids[:]).then_inc(pair_ready, 1)

            def tile_table():
                dve.wait_ge(rank_used, G)
                link(nc.vector.tensor_tensor(n_f[:], next_row[0:1, :], first_row[0:1, :], ALU.subtract))
                link(nc.vector.tensor_scalar(n_i[:], n_f[:], float(P - 1), None, ALU.add))
                link(nc.vector.tensor_scalar(n_i[:], n_i[:], P.bit_length() - 1, None, ALU.arith_shift_right))
                link(nc.vector.tensor_copy(n_f[:], n_i[:]))
                link(nc.vector.tensor_tensor_scan(n_end[:], ones[0:1, 0:E], n_f[:], 0.0, ALU.mult, ALU.add))
                shape = [1, SLOTS, E]
                link(nc.vector.tensor_tensor(past[:], tile_no[:, :, None].to_broadcast(shape),
                                             n_end[:, None, :].to_broadcast(shape), ALU.is_ge))
                link(nc.vector.tensor_tensor(past_n[:], past[:], n_f[:, None, :].to_broadcast(shape), ALU.mult),
                     nc.vector.tensor_reduce(t_exp[:], past[:], AX_X, ALU.add))
                link(nc.vector.tensor_reduce(t_start, past_n[:], AX_X, ALU.add),
                     nc.vector.scalar_tensor_tensor(out=t_row[:], in0=t_exp[:], scalar=float(EROWS // P), in1=tile_no,
                                                    op0=ALU.mult, op1=ALU.add))
                link(nc.vector.tensor_tensor(t_row[:], t_row[:], t_start, ALU.subtract),
                     nc.vector.tensor_scalar(tile_w[:], t_exp[:], float(E - 1), float(2 * EX_W), ALU.min, ALU.mult))
                link(nc.vector.tensor_scalar(t_exp[:], t_exp[:], float(E - 1), None, ALU.min))
                link(nc.vector.tensor_scalar(tile_need[:], t_exp[:], float(EX_PARTS), float(EX_PARTS), ALU.mult, ALU.add))
                link(nc.vector.tensor_copy(pad_row[:], next_row[0:1, :]))
                nc.vector.tensor_scalar(tile_row[:], t_row[:], float(E * EROWS // P), float(P), ALU.min, ALU.mult
                                        ).then_inc(tiles_ready, 1)

            def gated(g, m, up=UP):
                dve.wait_ge(silu_ready, SM * g + m + 1)
                if not isinstance(m, int) or SM * g + m > 0:
                    dve.wait_ge(hl_ready, SM * g + m)
                nc.vector.scalar_tensor_tensor(out=hm[:], in0=up, scalar=1 / WS, in1=silu[:], op0=ALU.mult,
                                               op1=ALU.mult).then_inc(hm_done, 1)
                dve.wait_ge(hh_ready, SM * g + m + 1)
                one = "p o t -> p (o t)"
                nc.vector.tensor_tensor(hTl[:, bass.ds(m, 1), :].rearrange(one), hm[:],
                                        hTh[:, bass.ds(m, 1), :].rearrange(one), ALU.subtract).then_inc(hl_ready, 1)

            def add_shared(g, q):
                dve.wait_ge(down_ready, Q * g + q + 1)
                r = x_tok[g % 3][:, q, :]
                nc.vector.scalar_tensor_tensor(out=r, in0=bank[4 + q % 2], scalar=1 / WS, in1=r, op0=ALU.mult,
                                               op1=ALU.add).then_inc(base_ready, 1)

            def mixed(g):
                for q in range(Q):
                    dve.wait_ge(outT_ready, Q * g + q + 1)
                    r = x_tok[g % 3][:, q, :]
                    nc.vector.scalar_tensor_tensor(out=r, in0=turn_bank("out", g, q), scalar=1 / WS, in1=r,
                                                   op0=ALU.mult, op1=ALU.add).then_inc(x1_done, 1)
                dve.wait_ge(x1_done, Q * (g + 1))
                moments(x_tok[g % 3])
                if g < G - 1:
                    total(HG * (g + 1), 0)
                normalise(x_tok[g % 3], 2 * g + 2 if g < G - 1 else 2 * G - 1, xf_ready)

            def expert_piece(e, c):
                at = e * (2 * EX_W) + c * EX_PIECE
                dve.wait_ge(piece_h, SH_PIECES + e * EX_PARTS + c + 1)
                nc.vector.scalar_tensor_tensor(
                    out=experts[:, bass.ds(at + EX_W, EX_PIECE)], in0=stage[c], scalar=WS,
                    in1=experts[:, bass.ds(at, EX_PIECE)], op0=ALU.mult, op1=ALU.subtract).then_inc(piece_l, 1)

            def expert(e, parts=range(EX_PARTS)):
                for c in parts:
                    expert_piece(e, c)

            value_moments(0)
            values(0)
            dve.wait_ge(const_in, 16)
            nc.vector.tensor_copy(next_row[:], first_row).then_inc(hm_done, 1)
            dve.wait_ge(gate_split_h, 1)
            nc.vector.scalar_tensor_tensor(out=gate_l[:], in0=gate_raw[:], scalar=WS, in1=gate_h[:], op0=ALU.mult,
                                           op1=ALU.subtract).then_inc(gate_split_l, 1)
            skip_product(0, 0)
            skip_term(0, 0)
            skip_term(0, 1)
            value_moments(1)
            low_parts(0, 0)
            for g in range(G):
                s0 = g * HG
                low_parts(s0 + 1, 1)
                products(s0, 0, g)
                if g == 0:
                    total(s0, 0)
                else:
                    mixed(g - 1)
                low_parts(s0 + 2, 0)
                products(s0 + 1, 1, g)
                if g > 0:
                    normed_low(g - 1, range(0, 2))
                total(s0 + 1, 1)
                if g == 0:
                    skip_term(0, 2)
                else:
                    normed_low(g - 1, range(2, 4))
                    if g < G - 1:
                        value_moments(g + 1)
                low_parts(s0 + 3, 1)
                finish(s0 + 2, 2, g)
                if g > 0:
                    pick(g - 1)
                    gated(g - 1, 0)
                else:
                    skip_term(0, 3)
                if g < G - 1:
                    values(g + 1)
                with dve.Fori(0, 2) as j:
                    for u in range(2):
                        h = 4 + 2 * j + u
                        low_parts(s0 + h, u)
                        finish(s0 + h - 1, h - 1, g)
                        if g > 0:
                            gated(g - 1, 1 + 2 * j + u)
                finish(s0 + HG - 1, HG - 1, g)
                if g > 0:
                    gated(g - 1, SM - 1)
                    pairs(g - 1)
                if g < G - 1:
                    skip_product(g + 1, 0)
                    for q in range(Q):
                        skip_term(g + 1, q)
                        if g > 0:
                            add_shared(g - 1, q)
                        if q == (1 if g > 0 else Q - 1):
                            low_parts(s0 + HG, 0)
            for c in range(EX_PARTS - 1):
                expert_piece(0, c)
            add_shared(G - 2, 0)
            add_shared(G - 2, 1)
            mixed(G - 1)
            add_shared(G - 2, 2)
            add_shared(G - 2, 3)
            normed_low(G - 1)
            expert_piece(0, EX_PARTS - 1)
            expert_piece(1, 0)
            pick(G - 1)
            expert(1, range(1, EX_PARTS))
            expert(2)
            ups = (UP, bank[1])
            gated(G - 1, 0)
            pairs(G - 1)
            tile_table()
            with dve.Fori(0, (SM - 2) // 2) as j:
                for u in range(2):
                    gated(G - 1, 1 + 2 * j + u, ups[(1 + u) % 2])
                    expert(3 + j, range(2 * u, 2 * u + 2))
            gated(G - 1, SM - 1, ups[(SM - 1) % 2])
            for e in range(early_experts, E):
                expert(e)
                if e < E - 1:
                    add_shared(G - 1, 2 * (e - early_experts))
                    add_shared(G - 1, 2 * (e - early_experts) + 1)

            def tile_low(t, par):
                dve.wait_ge(r_xh, t + 1)
                nc.vector.tensor_tensor(xgl[par], bank[2], xgh[par], ALU.subtract).then_inc(r_xl, 1)

            def tile_gated(t):
                dve.wait_ge(r_silu, t + 1)
                nc.vector.scalar_tensor_tensor(out=hm[:, 0:FF], in0=bank[1][:, 0:FF], scalar=1 / WS,
                                               in1=silu[:, 0:FF], op0=ALU.mult, op1=ALU.mult).then_inc(r_hm, 1)

            def tile_hidden_low(t):
                dve.wait_ge(r_hh, t + 1)
                nc.vector.tensor_tensor(hgl, bank[3][:, 0:FK * P], hgh, ALU.subtract).then_inc(r_hl, 1)

            tile_low(0, 0)
            tile_gated(0)
            tile_low(1, 1)
            tile_hidden_low(0)
            with dve.Fori(0, (TILES - 3) // 2) as j:
                for u in range(1, 3):
                    t = 2 * j + u
                    tile_gated(t)
                    tile_low(t + 1, (u + 1) % 2)
                    tile_hidden_low(t)
            for t in range(TILES - 2, TILES):
                tile_gated(t)
                if t + 1 < TILES:
                    tile_low(t + 1, (t + 1) % 2)
                tile_hidden_low(t)


def constants():
    import numpy as np

    con = np.zeros((P, CONST_W), np.float32)
    p = np.arange(P)
    con[:, 0:P] = np.eye(P)
    con[:, P:2 * P] = p[:, None] // NH == p[None, :] // NH
    con[:, 2 * P:3 * P] = p[:, None] < p[None, :]
    con[:, 3 * P:4 * P] = 1
    c = 4 * P
    con[:, c:c + 8] = np.arange(8)
    con[:, c + 8:c + 12] = -0.5
    con[:, c + 12:c + 20] = np.arange(E) * EROWS
    con[:, c + 20:c + 20 + SLOTS] = np.arange(SLOTS)
    con[:, c + 20 + SLOTS:] = (np.arange(Q)[None] * 2 + p[:, None] // RG) * S + p[:, None] % RG
    table = np.zeros((TROWS, 2), np.int32)
    table[:, 0] = T + np.arange(TROWS) % P
    return con, table, np.zeros((P, L), np.float32)


def kernel(x, fside_S2_0, ctx_2048, L0_xattn_k, L0_ffn_gate_w, L0_ffn_shared_wg, L0_ffn_shared_wu, L0_ffn_shared_wd,
           L0_ffn_exp_wg, L0_ffn_exp_wu, L0_ffn_exp_wd):
    import numpy as np
    import concourse.bacc as bacc
    from concourse.bass_utils import run_bass_kernel_spmd

    def rows(w, n):
        w = w.reshape(*w.shape[:-2], n, P, w.shape[-1])
        w = np.moveaxis(w, -3, -2)
        return w.reshape(*w.shape[:-2], n * w.shape[-1])

    def padded(w, n):
        return np.concatenate([w, np.zeros((*w.shape[:-1], n - w.shape[-1]), w.dtype)], -1)

    a = {k: np.asarray(v) for k, v in dict(
        x=x, skip=fside_S2_0, ctx=ctx_2048, k=L0_xattn_k, gate=L0_ffn_gate_w, sg=L0_ffn_shared_wg, su=L0_ffn_shared_wu,
        sd=L0_ffn_shared_wd, eg=L0_ffn_exp_wg, eu=L0_ffn_exp_wu, ed=L0_ffn_exp_wd).items()}
    con, table, zeros = constants()
    gu = np.concatenate([padded(a["sg"].T, SFP), padded(a["su"].T, SFP)], -1)
    sd = padded(a["sd"], SFP).T
    ed = a["ed"]
    whole = (FK - 1) * P
    last = np.concatenate([np.zeros((E, L, FK * P - FF), ed.dtype), ed[:, :, whole:]], -1)
    ed = np.concatenate([ed[:, :, 0:whole], last], -1)
    t = lambda w: np.swapaxes(w, -1, -2)
    arrays = {
        "x": a["x"], "ctx": a["ctx"],
        "ctx_hidden": a["ctx"].reshape(B, G, RG, LB, P).transpose(1, 4, 3, 0, 2).reshape(G, P, LB * TG),
        "skip": np.tile(a["skip"].reshape(G, RG).T, (2, 1)),
        "krev": padded(a["k"][:, ::-1], KREV),
        "gate_w": rows(a["gate"].T, LB),
        "shared_w": np.concatenate([rows(sd, SM), rows(gu, LB)], -1),
        "expert_w": np.concatenate([rows(t(a["eg"]), LB), rows(t(a["eu"]), LB), rows(t(ed), FK)], -1),
        "consts": con, "table0": table, "zeros": zeros,
    }
    arrays = {f"in_{k}": np.ascontiguousarray(v) for k, v in arrays.items()}
    nc = bacc.Bacc("TRN2", target_bir_lowering=False, num_devices=1)
    args = [nc.dram_tensor(k, v.shape, mybir.dt.from_np(v.dtype), kind="ExternalInput").ap() for k, v in arrays.items()]
    out = nc.dram_tensor("out", (T + P, L), F32, kind="ExternalOutput").ap()
    xattn_moe(nc, *args, out)
    r = run_bass_kernel_spmd(nc, [arrays], core_ids=[0])
    return r.results[0]["out"][0:T].reshape(B, S, L)
```

```python
from contextlib import ExitStack

import concourse.bass as bass
from concourse import mybir

ALU = mybir.AluOpType
ACT = mybir.ActivationFunctionType
AX_X = mybir.AxisListType.X
F32 = mybir.dt.float32
F16 = mybir.dt.float16
I32 = mybir.dt.int32
U32 = mybir.dt.uint32

P = 128
B, S, L = 8, 256, 512
NH = 8
H = S // NH
LB = L // P
HG = 8
G = H // HG
RG = HG * NH
TG = B * RG
Q = TG // P
T = B * S
COLS = B * NH * NH
E = 8
FF = 352
FK = -(-FF // P)
SFF = 704
SM = -(-SFF // P)
HALF = SFF % P
SH_GU = LB * 2 * SFF
SH_W = SH_GU + SM * L
SH_PIECE = 1024
SH_PIECES = -(-SH_W // SH_PIECE)
EX_W = 2 * LB * FF + FK * L
EX_PARTS = 4
EX_PIECE = EX_W // EX_PARTS
TILES = 2 * T // P + E - 1
EROWS = T + P
TROWS = E * EROWS + P
RING = 4
EPS = 1e-5
ROUTE_SCALE = 2.5
WS = 256.0
SLOTS = -(-TILES // RING) * RING
CONST_W = 4 * P + 20 + SLOTS + Q + 1
KREV = L + P


def xattn_moe(nc, x, ctx, ctx_hidden, skip, krev, gate_w, shared_w, expert_w, consts, table0, zeros, out):
    scaled = nc.dram_tensor("scaled_filters", [H, KREV], F32).ap()
    filters = bass.AP(scaled.tensor, 0, [[KREV, H], [1, P], [1, L]])
    x_rows = x.rearrange("b (g r) l -> g b r l", r=RG)
    ctx_rows = ctx.rearrange("b (g r) l -> g b r l", r=RG)
    out_rows = out[0:T, :].rearrange("(b g r) l -> g b r l", b=B, g=G)
    pair_rows = nc.dram_tensor("pair_rows", [TROWS, L], F32).ap()
    table = nc.dram_tensor("pair_table", [TROWS, 2], I32).ap()

    with ExitStack() as stack:
        def sb(name, shape, dt):
            return stack.enter_context(nc.sbuf_tensor(name, shape, dt))

        def sem(name):
            return stack.enter_context(nc.semaphore(name))

        ps = stack.enter_context(nc.psum_tensor("banks", [P, 8, 512], F32))

        arena = sb("arena", [P, E * EX_W], F32)
        place = [0]

        def carve(words):
            place[0] += words
            return arena[:, place[0] - words:place[0]]

        kv = [carve(LB * COLS) for _ in range(2)]
        kvh = [carve(LB * COLS // 2).bitcast(F16) for _ in range(2)]
        kvl = [carve(LB * COLS // 2).bitcast(F16) for _ in range(2)]
        prod = carve(LB * COLS)
        vT = [carve(LB * TG) for _ in range(2)]
        cT = [carve(LB * TG) for _ in range(2)]
        filt_raw = [carve(L) for _ in range(2)]
        fh = [carve(L // 2).bitcast(F16) for _ in range(2)]
        fl = [carve(L // 2).bitcast(F16) for _ in range(2)]
        ctx_tok = carve(Q * L).rearrange("p (q l) -> p q l", q=Q)
        x_tok2 = carve(Q * L).rearrange("p (q l) -> p q l", q=Q)
        filt_all = prod[0:H, 0:KREV]
        place[0] = E * EX_W - SH_W
        shared_gu = carve(SH_GU)
        shared_d = carve(SH_W - SH_GU)
        gu_h, gu_l = shared_gu[:, 0:SH_GU // 2].bitcast(F16), shared_gu[:, SH_GU // 2:SH_GU].bitcast(F16)
        d_n = SH_W - SH_GU
        d_h, d_l = shared_d[:, 0:d_n // 2].bitcast(F16), shared_d[:, d_n // 2:d_n].bitcast(F16)
        experts = arena[:, :].bitcast(F16)

        x_tok = [sb(f"x_tok{i}", [P, Q, L], F32) for i in range(2)] + [x_tok2]
        normed = sb("normed", [P, Q, L], F32)
        mixT = sb("mixT", [P, LB * TG], F32)
        xfh = sb("xfh", [P, LB, TG], F16)
        xfl = sb("xfl", [P, LB, TG], F16)
        silu = sb("silu", [P, 512], F32)
        hm = sb("hm", [P, 512], F32)
        skipped = [hm, silu]
        hTh = sb("hTh", [P, SM, TG], F16)
        hTl = sb("hTl", [P, SM, TG], F16)
        stages = sb("stages", [P, 2 * EX_PIECE], F32)
        stage = [stages[:, 0:EX_PIECE], stages[:, EX_PIECE:2 * EX_PIECE],
                 x_tok[1].rearrange("p q l -> p (q l)")[:, 0:EX_PIECE], mixT[:, 0:EX_PIECE]]
        early = [e * EX_W + EX_W for e in range(3)]

        def raw_piece(e, c):
            if isinstance(e, int) and 1 <= e <= 2:
                return arena[:, early[e] + c * EX_PIECE:early[e] + (c + 1) * EX_PIECE]
            return stage[c]

        kept = [stages[:, 0:Q * L].rearrange("p (q l) -> p q l", q=Q)] * 2 + [ctx_tok, normed]
        con = sb("con", [P, CONST_W], F32)
        ident, block8, before, ones = (con[:, i * P:(i + 1) * P] for i in range(4))
        iota8 = con[:, 4 * P:4 * P + 8]
        minus_half = con[:, 4 * P + 8:4 * P + 12]
        first_row = con[:, 4 * P + 12:4 * P + 20]
        tile_no = con[0:1, 4 * P + 20:4 * P + 20 + SLOTS]
        part_no = con[:, CONST_W - 1:CONST_W]
        row_base = con[:, 4 * P + 20 + SLOTS:CONST_W - 1]
        tok_ids = sb("tok_ids", [P, Q], I32)
        skip_col = sb("skip_col", [P, G], F32)
        gate_raw = sb("gate_raw", [P, LB * E], F32)
        gate_h = sb("gate_h", [P, LB * E], F16)
        gate_l = sb("gate_l", [P, LB * E], F16)
        stats = sb("stats", [P, Q, 6], F32)
        meanvar = sb("meanvar", [P, Q, 2], F32)
        var_eps = sb("var_eps", [P, Q], F32)
        rstd = sb("rstd", [P, Q], F32)
        shift = sb("shift", [P, Q], F32)
        score = sb("score", [P, Q, E], F32)
        top = sb("top", [P, Q, E], F32)
        topi = sb("topi", [P, Q, E], U32)
        topf = sb("topf", [P, Q, 2], F32)
        onehot = sb("onehot", [P, Q, 2, E], F32)
        picked = sb("picked", [P, Q + 1, E], F16)
        masks16 = sb("masks16", [P, 2 * P], F16)
        before16, ones16 = masks16[:, 0:P], masks16[:, P:2 * P]
        rank = sb("rank", [P, Q, E], F32)
        rankhot = sb("rankhot", [P, Q, 2, E], F32)
        rowf = sb("rowf", [P, Q, 2], F32)
        row = sb("row", [P, Q, 2], I32)
        pair = sb("pair", [P, Q, 2, 2], I32)
        wsum = sb("wsum", [P, Q], F32)
        winv = sb("winv", [P, Q], F32)
        wtop = sb("wtop", [P, Q, 2], F32)
        next_row = sb("next_row", [P, E], F32)
        n_i = sb("n_i", [1, E], I32)
        n_f = sb("n_f", [1, E], F32)
        n_end = sb("n_end", [1, E], F32)
        pad_row = sb("pad_row", [P, E], I32)
        past, past_n = (mixT[0:1, EX_PIECE + i * SLOTS * E:EX_PIECE + (i + 1) * SLOTS * E]
                        .rearrange("p (t e) -> p t e", e=E) for i in range(2))
        t_start = mixT[0:1, EX_PIECE + 2 * SLOTS * E:EX_PIECE + 2 * SLOTS * E + SLOTS]
        t_exp = sb("t_exp", [1, SLOTS], F32)
        t_row = sb("t_row", [1, SLOTS], F32)
        tile_row = sb("tile_row", [1, SLOTS], I32)
        tile_w = sb("tile_w", [1, SLOTS], I32)
        tile_need = sb("tile_need", [1, SLOTS], I32)
        ids = [sb(f"ids{i}", [P, 2], I32) for i in range(RING)]
        xg = [normed[:, i, :] for i in range(RING)]
        yg = [x_tok[0][:, i, :] for i in range(RING)]
        xgh = [xfh[:, i, :] for i in range(2)]
        xgl = [xfl[:, i, :] for i in range(2)]
        hgh = xfh[:, 2, 0:FK * P]
        hgl = xfl[:, 2, 0:FK * P]

        const_in = sem("const_in")
        small_in = sem("small_in")
        x_in = [sem(f"x_in{g}") for g in range(G)]
        ctx_in = [sem(f"ctx_in{g}") for g in range(G)]
        cT_in = [sem(f"cT_in{g}") for g in range(G)]
        filt_all_in = sem("filt_all_in")
        filt_scaled = sem("filt_scaled")
        filt_stored = sem("filt_stored")
        filt_in = [sem(f"filt_in{i}") for i in range(2)]
        stage_in = [sem(f"stage_in{i}") for i in range(RING)]
        early_in = [[sem(f"early_in{e}{c}") for c in range(EX_PARTS)] for e in range(1, 3)]
        init_done = sem("init_done")
        base_stored = sem("base_stored")
        rows_kept = sem("rows_kept")
        rows_sent = sem("rows_sent")
        pads_sent = sem("pads_sent")
        pairs_stored = sem("pairs_stored")
        ids_in = [sem(f"ids_in{i}") for i in range(RING)]
        rows_in = [sem(f"rows_in{i}") for i in range(RING)]
        added = sem("added")
        kv_ready = sem("kv_ready")
        fh_ready = sem("fh_ready")
        fl_ready = sem("fl_ready")
        kvh_ready = sem("kvh_ready")
        kvl_ready = sem("kvl_ready")
        conv_ready = sem("conv_ready")
        prod_done = sem("prod_done")
        mix_done = sem("mix_done")
        v_ready = sem("v_ready")
        skip_ready = sem("skip_ready")
        tokT_ready = sem("tokT_ready")
        tokT_done = sem("tokT_done")
        skipsum_ready = sem("skipsum_ready")
        skip_done = sem("skip_done")
        var_ready = sem("var_ready")
        rstd_ready = sem("rstd_ready")
        v_shift_ready = sem("v_shift_ready")
        shift_ready = sem("shift_ready")
        outT_ready = sem("outT_ready")
        x1_done = sem("x1_done")
        xf_ready = sem("xf_ready")
        xfT_ready = sem("xfT_ready")
        xfh_ready = sem("xfh_ready")
        xfl_ready = sem("xfl_ready")
        logit_ready = sem("logit_ready")
        score_ready = sem("score_ready")
        picked_ready = sem("picked_ready")
        rank_ready = sem("rank_ready")
        rank_used = sem("rank_used")
        pair_ready = sem("pair_ready")
        gu_ready = sem("gu_ready")
        silu_ready = sem("silu_ready")
        hm_done = sem("hm_done")
        hh_ready = sem("hh_ready")
        hl_ready = sem("hl_ready")
        down_ready = sem("down_ready")
        base_ready = sem("base_ready")
        piece_h = sem("piece_h")
        shared_l = sem("shared_l")
        piece_l = sem("piece_l")
        gate_split_h = sem("gate_split_h")
        gate_split_l = sem("gate_split_l")
        tiles_ready = sem("tiles_ready")
        dve_step = sem("dve_step")
        pool_passed = sem("pool_passed")
        r_gu = sem("r_gu")
        r_silu = sem("r_silu")
        r_hm = sem("r_hm")
        r_xT = sem("r_xT")
        r_xh = sem("r_xh")
        r_xl = sem("r_xl")
        r_hT = sem("r_hT")
        r_hh = sem("r_hh")
        r_hl = sem("r_hl")
        r_down = sem("r_down")
        r_y = sem("r_y")

        bank = [ps[:, i, :] for i in range(8)]
        GATE, UP = bank[4], bank[5]

        def turns_of(name, g):
            if name == "prep":
                for q in range(Q):
                    yield tokT_done, Q * g + q + 1
                for q in range(Q):
                    yield skip_done, Q * g + q + 1
            elif name == "out":
                for q in range(Q):
                    yield x1_done, Q * g + q + 1
            elif name == "xf":
                for q in range(Q):
                    yield xfl_ready, Q * g + q + 1
                yield score_ready, g + 1
            elif name == "rank":
                yield rank_used, g + 1

        turn_order = [("prep", 0)]
        for g in range(G):
            turn_order += [("out", g - 1), ("xf", g - 1)] if g > 0 else []
            turn_order += [("rank", g - 1)] if 0 < g < G - 1 else []
            turn_order += [("prep", g + 1)] if g < G - 1 else []
        turn_order += [("out", G - 1), ("rank", G - 2), ("xf", G - 1), ("rank", G - 1)]
        turn_read = [t for name, g in turn_order for t in turns_of(name, g)]

        def turn_bank(name, g, k):
            n = sum(len(list(turns_of(*w))) for w in turn_order[:turn_order.index((name, g))])
            return bank[6 + (n + k) % 2]

        def backwards(v):
            return bass.AP(v.tensor, v.offset + L - 1, [v.ap[0], [-1, L]])

        def heads(v):
            return v.rearrange("p (a r) -> p a r", r=RG)

        def shared_width(i):
            return min(SH_PIECE, SH_W - i * SH_PIECE) if isinstance(i, int) else SH_PIECE

        def shared_piece(i, down, gate_up):
            down_pieces = d_n // SH_PIECE
            if isinstance(i, int) and i < down_pieces:
                return down[:, i * SH_PIECE:(i + 1) * SH_PIECE]
            return gate_up[:, bass.ds((i - down_pieces) * SH_PIECE, shared_width(i))]

        def down_bank(g, q):
            return bank[4 + (q if isinstance(g, int) and g == G - 1 else q % 2)]

        def half_tile(m):
            return isinstance(m, int) and m == 0

        half = EX_PARTS // 2
        first_half, second_half = tuple(range(half)), tuple(range(half, EX_PARTS))
        split_after = (4, 2, 2, 0, 2, 2)
        pieces_after = [[divmod(i, EX_PARTS) for i in range(2 * EX_PARTS + sum(split_after[:m]),
                                                            2 * EX_PARTS + sum(split_after[:m + 1]))]
                        for m in range(SM)]

        block = stack.enter_context(nc.Block())


        @block.sync
        def _(sp):
            def load_filter(s, par):
                sp.dma_start(filt_raw[par], filters[bass.ds(s, 1), :, :].rearrange("o p l -> (o p) l")
                             ).then_inc(filt_in[par], 16)

            def next_filter(s, par):
                sp.wait_ge(fl_ready, s - 1)
                load_filter(s, par)

            def load_rows(dst, src, done):
                for b2 in range(2):
                    sp.dma_start(dst[b2 * RG:(b2 + 1) * RG, :, :],
                                 src.rearrange("(q t) r l -> t r q l", t=2)[b2]).then_inc(done, 16)

            def load_context(g):
                sp.wait_ge(skip_done, Q * g)
                load_rows(ctx_tok, ctx_rows[g], ctx_in[g])

            def load_hidden(g):
                sp.dma_start(cT[g % 2], ctx_hidden[g]).then_inc(cT_in[g], 16)

            def store(dst, src, done):
                for b2 in range(2):
                    sp.dma_start(dst.rearrange("(q t) r l -> t r q l", t=2)[b2],
                                 src[b2 * RG:(b2 + 1) * RG, :, :]).then_inc(done, 16)

            def load_shared(i, par):
                sp.dma_start(stage[par][:, 0:SH_PIECE], shared_w[:, bass.ds(i * SH_PIECE, SH_PIECE)]
                             ).then_inc(stage_in[par], 16)

            def next_shared(i, par):
                sp.wait_ge(shared_l, i - 1)
                load_shared(i, par)

            def load_piece(e, c):
                done = early_in[e - 1][c] if isinstance(e, int) and 1 <= e <= 2 else stage_in[c]
                sp.dma_start(raw_piece(e, c), expert_w[bass.ds(e, 1), :, c * EX_PIECE:(c + 1) * EX_PIECE]
                             .rearrange("e p n -> (e p) n")).then_inc(done, 16)

            def load_expert(e, *parts):
                before = 0 if isinstance(e, int) and e == 3 else e - 1
                for c in parts or range(EX_PARTS):
                    sp.wait_ge(piece_l, before * EX_PARTS + c + 1)
                    load_piece(e, c)

            load_rows(x_tok[0], x_rows[0], x_in[0])
            sp.dma_start(con[:], consts).then_inc(const_in, 16)
            sp.dma_start(filt_all, krev).then_inc(filt_all_in, 16)
            sp.dma_start(skip_col[:], skip).then_inc(small_in, 16)
            sp.dma_start(gate_raw[:], gate_w).then_inc(small_in, 16)
            load_rows(ctx_tok, ctx_rows[0], ctx_in[0])
            sp.wait_ge(filt_scaled, 1)
            sp.dma_start(scaled, filt_all).then_inc(filt_stored, 16)
            load_rows(x_tok[1], x_rows[1], x_in[1])
            load_hidden(0)
            sp.wait_ge(filt_stored, 16)
            load_filter(0, 0)
            load_filter(1, 1)
            sp.wait_ge(cT_in[0], 16)
            load_shared(0, 0)
            load_shared(1, 1)
            sp.dma_start(table, table0).then_inc(init_done, 16)
            sp.dma_start(pair_rows[E * EROWS:TROWS, :], zeros).then_inc(init_done, 16)
            sp.dma_start(out[T:T + P, :], zeros).then_inc(init_done, 16)
            for g in range(G):
                s0 = g * HG
                next_filter(s0 + 2, 0)
                next_filter(s0 + 3, 1)
                if g == 0:
                    next_shared(2, 0)
                    load_hidden(1)
                    load_context(1)
                elif g < G - 1:
                    if g >= 2:
                        sp.wait_ge(base_stored, 32 * (g - 1))
                    load_rows(x_tok[(g + 1) % 3], x_rows[g + 1], x_in[g + 1])
                    load_context(g + 1)
                    sp.wait_ge(mix_done, HG * g)
                    load_hidden(g + 1)
                if g > 0:
                    if g == 1:
                        sp.wait_ge(shared_l, SH_PIECES)
                    elif g == 2:
                        sp.wait_ge(rows_sent, 16 * 2 * Q)
                    sp.wait_ge(xf_ready, Q * g)
                    sp.dma_start(kept[g - 1], normed[:]).then_inc(rows_kept, 16)
                for h in range(4, 6):
                    next_filter(s0 + h, h % 2)
                    if g == 0:
                        next_shared(h - 1, (h - 1) % 2)
                with sp.Fori(0, 2 if g < G - 1 else 1) as j:
                    for u in range(2):
                        next_filter(s0 + 6 + 2 * j + u, u)
                        if g == 0:
                            next_shared(5 + 2 * j + u, (1 + u) % 2)
                if 0 < g < G - 1:
                    sp.wait_ge(base_ready, Q * g)
                    store(out_rows[g - 1], x_tok[(g - 1) % 3], base_stored)
            sp.wait_ge(rows_sent, 16 * 2 * Q * 2)
            load_piece(0, 0)
            load_piece(0, 1)
            sp.wait_ge(base_stored, 32 * 2)
            load_piece(0, 2)
            sp.wait_ge(mix_done, H)
            for c in range(EX_PARTS):
                load_piece(1, c)
            sp.wait_ge(outT_ready, Q * G)
            load_piece(0, 3)
            for c in range(EX_PARTS):
                load_piece(2, c)
            load_expert(3)
            sp.wait_ge(base_ready, Q * (G - 1))
            store(out_rows[G - 2], x_tok[(G - 2) % 3], base_stored)
            load_expert(E - 4)
            load_expert(E - 3)

            def load_tile(t, slot):
                r = sp.value_load(tile_row[0:1, bass.ds(t, 1)], min_val=0, max_val=TROWS - P)
                sp.dma_start(xg[slot], pair_rows[bass.ds(r, P), :]).then_inc(rows_in[slot], 16)
                sp.dma_start(ids[slot][:], table[bass.ds(r, P), :]).then_inc(ids_in[slot], 16)

            sp.wait_ge(tiles_ready, 1)
            sp.wait_ge(pads_sent, 16 * E)
            sp.wait_ge(rows_sent, 16 * 2 * Q * G)
            sp.wait_ge(pairs_stored, 16 * 2 * Q * G)
            for t in range(RING):
                load_tile(t, t)
                if t < 2:
                    load_expert(E - 2, *(first_half, second_half)[t])
            load_expert(E - 1)
            sp.wait_ge(base_ready, Q * G)
            store(out_rows[G - 1], x_tok[(G - 1) % 3], base_stored)
            with sp.Fori(0, TILES // RING - 1) as j:
                for u in range(RING):
                    sp.wait_ge(added, 16 * (j * RING + u + 1))
                    load_tile(RING + j * RING + u, u)
            for t in range(TILES // RING * RING, TILES):
                sp.wait_ge(added, 16 * (t - RING + 1))
                load_tile(t, t % RING)
            sp.wait_ge(base_stored, 32 * G)
            sp.wait_ge(init_done, 48)
            sp.wait_ge(added, 16 * TILES)

        @block.gpsimd
        def _(pool):
            def outer(s, h, g, par):
                v = heads(vT[g % 2])[:, :, bass.ds(h * NH, NH)]
                c = heads(cT[g % 2])[:, :, bass.ds(h * NH, NH)]
                shape = [P, LB * B, NH, NH]
                nc.gpsimd.tensor_tensor(kv[par].rearrange("p (a i j) -> p a i j", i=NH, j=NH),
                                        v[:, :, :, None].to_broadcast(shape), c[:, :, None, :].to_broadcast(shape),
                                        ALU.mult).then_inc(kv_ready, 1)

            def inverse_root(n):
                pool.wait_ge(var_ready, n + 1)
                nc.gpsimd.tensor_tensor(rstd[:], var_eps[:], minus_half, ALU.pow).then_inc(rstd_ready, 1)

            def place(q, k):
                return bass.IndirectOffsetOnAxis(ap=row[:, q, k:k + 1], axis=0)

            def send_rows(g):
                pool.wait_ge(pair_ready, g + 1)
                if g < G - 1:
                    pool.wait_ge(rows_kept, 16 * (g + 1))
                for q in range(Q):
                    for k in range(2):
                        nc.gpsimd.indirect_dma_start(out=pair_rows, out_offset=place(q, k), in_=kept[g][:, q, :],
                                                     in_offset=None).then_inc(rows_sent, 16)

            def send_pads():
                for e in range(E):
                    behind = bass.IndirectOffsetOnAxis(ap=pad_row[:, e:e + 1], axis=0)
                    nc.gpsimd.indirect_dma_start(out=pair_rows, out_offset=behind, in_=normed[:, 0, :],
                                                 in_offset=None).then_inc(pads_sent, 16)

            def send_pairs():
                for q in range(Q):
                    for k in range(2):
                        nc.gpsimd.indirect_dma_start(out=table, out_offset=place(q, k), in_=pair[:, q, k, :],
                                                     in_offset=None).then_inc(pairs_stored, 16)

            def filter_low(s, par):
                pool.wait_ge(fh_ready, s + 1)
                nc.gpsimd.tensor_tensor(fl[par], backwards(filt_raw[par]), fh[par], ALU.subtract).then_inc(fl_ready, 1)

            def piece(i, par):
                width = shared_width(i)
                pool.wait_ge(piece_h, i + 1)
                nc.gpsimd.tensor_tensor(shared_piece(i, d_l, gu_l), stage[par][:, 0:width], shared_piece(i, d_h, gu_h),
                                        ALU.subtract).then_inc(shared_l, 1)

            pool.wait_ge(const_in, 16)
            inverse_root(0)
            pool.wait_ge(tokT_done, Q)
            pool.wait_ge(cT_in[0], 16)
            outer(0, 0, 0, 0)
            filter_low(0, 0)
            outer(1, 1, 0, 1)
            filter_low(1, 1)
            for g in range(G):
                s0 = g * HG
                pool.wait_ge(kvl_ready, s0 + 1)
                outer(s0 + 2, 2, g, 0)
                if g == 0:
                    piece(0, 0)
                inverse_root(2 * g if g > 0 else 1)
                filter_low(s0 + 2, 0)
                pool.wait_ge(kvl_ready, s0 + 2)
                outer(s0 + 3, 3, g, 1)
                if g == 0:
                    piece(1, 1)
                filter_low(s0 + 3, 1)
                if g == 0:
                    piece(2, 0)
                elif g >= 2:
                    send_pairs()
                with pool.Fori(0, 2) as j:
                    for u in range(2):
                        pool.wait_ge(kvl_ready, s0 + 3 + 2 * j + u)
                        outer(s0 + 4 + 2 * j + u, 4 + 2 * j + u, g, u)
                        if g == 0:
                            piece(3 + 2 * j + u, (1 + u) % 2)
                        filter_low(s0 + 4 + 2 * j + u, u)
                if 0 < g < G - 1:
                    inverse_root(2 * g + 1)
                if g < G - 1:
                    pool.wait_ge(tokT_done, Q * (g + 2))
                    pool.wait_ge(cT_in[g + 1], 16)
                    for h in range(2):
                        pool.wait_ge(kvl_ready, s0 + HG + h - 1)
                        outer(s0 + HG + h, h, g + 1, h)
                        filter_low(s0 + HG + h, h)
                if g == 0:
                    piece(7, 1)
                    piece(8, 0)
                    pool.wait_ge(init_done, 48)
                elif g < G - 1:
                    send_rows(g - 1)
            inverse_root(2 * G - 1)
            send_rows(G - 2)
            send_pairs()
            send_rows(G - 1)
            send_pads()
            send_pairs()

            def add_tile(t, slot):
                pool.wait_ge(r_y, t + 1)
                if not isinstance(t, int) or t > 0:
                    pool.wait_ge(added, 16 * t)
                pool.sem_inc(pool_passed, 1)
                pool.wait_ge(base_stored, 32 * G)
                nc.gpsimd.indirect_dma_start(
                    out=out, out_offset=bass.IndirectOffsetOnAxis(ap=ids[slot][:, 0:1], axis=0),
                    in_=yg[slot], in_offset=None, compute_op=ALU.add).then_inc(added, 16)

            add_tile(0, 0)
            with pool.Fori(0, (TILES - 3) // RING) as j:
                for u in range(1, RING + 1):
                    add_tile(RING * j + u, u % RING)
            for t in range(TILES - 2, TILES):
                add_tile(t, t % RING)

        @block.tensor
        def _(pe):
            turn = [0]

            def take():
                k = turn[0]
                turn[0] += 1
                if k >= 2:
                    pe.wait_ge(*turn_read[k - 2])
                return bank[6 + k % 2]

            def split_products(dst, w, x, n, first=0, end=None):
                for k in range(first, end or n):
                    (wh, wl), (xh, xl) = w(k), x(k)
                    nc.tensor.matmul(dst, wh, xh, start=(k == 0), stop=False)
                    nc.tensor.matmul(dst, wh, xl, start=False, stop=False)
                    last = nc.tensor.matmul(dst, wl, xh, start=False, stop=(k == n - 1))
                return last

            def convolve(s, par, first=False, blocks=range(LB)):
                if blocks[0] == 0:
                    pe.wait_ge(kvl_ready, s + 1)
                    pe.wait_ge(fl_ready, s + 1)
                for n in blocks:
                    if not first:
                        pe.wait_ge(prod_done, LB * s - LB + 1 + n)
                    last = split_products(
                        bank[n],
                        lambda m: (fh[par][:, (n - m) * P:(n - m + 1) * P], fl[par][:, (n - m) * P:(n - m + 1) * P]),
                        lambda m: (kvh[par][:, m * COLS:(m + 1) * COLS], kvl[par][:, m * COLS:(m + 1) * COLS]), n + 1)
                    last.then_inc(conv_ready, 1)

            def transpose_tile(dst, src, done):
                for lb in range(LB):
                    last = nc.tensor.transpose(dst[:, lb * P:(lb + 1) * P], src(lb), ident)
                last.then_inc(done, 1)

            def prepare(g):
                for q in range(Q):
                    t = take()
                    pe.wait_ge(v_ready, Q * g + q + 1)
                    transpose_tile(t, lambda lb: normed[:, q, lb * P:(lb + 1) * P], tokT_ready)

            def skip_sum(g, q):
                t = take()
                pe.wait_ge(skip_ready, Q * g + q + 1)
                nc.tensor.matmul(t, block8, skipped[q % 2][:], start=True, stop=True).then_inc(skipsum_ready, 1)

            def mix_out(g, tiles=range(Q)):
                pe.wait_ge(mix_done, HG * (g + 1))
                for q in tiles:
                    transpose_tile(take(), lambda lb: mixT[:, lb * TG + q * P:lb * TG + (q + 1) * P], outT_ready)

            def normed_out(g, q):
                t = take()
                pe.wait_ge(xf_ready, Q * g + q + 1)
                transpose_tile(t, lambda lb: normed[:, q, lb * P:(lb + 1) * P], xfT_ready)

            def logits(g):
                t = take()
                pe.wait_ge(xfl_ready, Q * (g + 1))
                pe.wait_ge(gate_split_l, 1)
                for q in range(Q):
                    last = split_products(
                        t[:, q * E:(q + 1) * E],
                        lambda lb: (xfh[:, lb, q * P:(q + 1) * P], xfl[:, lb, q * P:(q + 1) * P]),
                        lambda lb: (gate_h[:, lb * E:(lb + 1) * E], gate_l[:, lb * E:(lb + 1) * E]), LB)
                last.then_inc(logit_ready, 1)

            def ranks(g):
                t = take()
                pe.wait_ge(picked_ready, g + 1)
                nc.tensor.matmul(t[:, 0:(Q + 1) * E], before16, picked[:].rearrange("p q e -> p (q e)"), start=True, stop=False)
                for k in range(Q):
                    last = nc.tensor.matmul(t[:, (k + 1) * E:(Q + 1) * E].rearrange("p (q e) -> p q e", e=E), ones16,
                                            picked[:, k:k + 1, :].to_broadcast([P, Q - k, E]), start=False,
                                            stop=(k == Q - 1))
                last.then_inc(rank_ready, 1)

            def gate_up(g, m, banks=(GATE, UP), ahead=0):
                pe.wait_ge(hm_done, SM * g + m + 1 - ahead)
                if g > 0:
                    pe.wait_ge(base_ready, Q * g)
                for half, dst in enumerate(banks[0:1] if half_tile(m) else banks):
                    def weights(lb):
                        c = bass.ds(lb * 2 * SFF + half * (SFF - HALF) + m * P, P)
                        return gu_h[:, c], gu_l[:, c]

                    last = split_products(dst, weights, lambda lb: (xfh[:, lb, :], xfl[:, lb, :]), LB)
                last.then_inc(gu_ready, 1)

            def down(g, q, first=0, end=SM):
                if q >= 2 and g < G - 1 and first == 0:
                    pe.wait_ge(base_ready, Q * g + q - 1)
                rows = [slice(0, HALF if half_tile(k) else P) for k in range(SM)]
                terms = (down_bank(g, q),
                         lambda k: (hTh[rows[k], k, q * P:(q + 1) * P], hTl[rows[k], k, q * P:(q + 1) * P]),
                         lambda k: (d_h[rows[k], k * L:(k + 1) * L], d_l[rows[k], k * L:(k + 1) * L]), SM)
                if q == 0:
                    pe.wait_ge(hm_done, SM * (g + 1) + (1 if g < G - 1 else 0))
                    pe.wait_ge(hl_ready, SM * (g + 1) - 1)
                    split_products(*terms, end=SM - 1)
                    pe.wait_ge(hl_ready, SM * (g + 1))
                    last = split_products(*terms, first=SM - 1)
                else:
                    last = split_products(*terms, first=first, end=end)
                if end == SM:
                    last.then_inc(down_ready, 1)

            pe.wait_ge(const_in, 16)
            prepare(0)
            for q in range(Q):
                skip_sum(0, q)
            for g in range(G):
                s0 = g * HG
                convolve(s0, 0, first=(g == 0))
                if g > 0:
                    mix_out(g - 1)
                convolve(s0 + 1, 1)
                if g == 1:
                    pe.wait_ge(shared_l, SH_PIECES)
                if g > 0:
                    normed_out(g - 1, 0)
                    normed_out(g - 1, 1)
                if g > 0:
                    convolve(s0 + 2, 0, blocks=range(0, LB - 1))
                    normed_out(g - 1, 2)
                    normed_out(g - 1, 3)
                    convolve(s0 + 2, 0, blocks=range(LB - 1, LB))
                    logits(g - 1)
                    gate_up(g - 1, 0)
                else:
                    convolve(s0 + 2, 0)
                    prepare(1)
                    skip_sum(1, 0)
                    skip_sum(1, 1)
                convolve(s0 + 3, 1)
                if g > 0:
                    gate_up(g - 1, 1)
                else:
                    skip_sum(1, 2)
                    skip_sum(1, 3)
                with pe.Fori(0, 2) as j:
                    for u in range(2):
                        convolve(s0 + 4 + 2 * j + u, u)
                        if g > 0:
                            gate_up(g - 1, 2 + 2 * j + u)
                if 0 < g < G - 1:
                    ranks(g - 1)
                    down(g - 1, 0)
                    down(g - 1, 1)
                    prepare(g + 1)
                    skip_sum(g + 1, 0)
                    down(g - 1, 2)
                    skip_sum(g + 1, 1)
                    skip_sum(g + 1, 2)
                    down(g - 1, 3)
                    skip_sum(g + 1, 3)
            mix_out(G - 1, range(0, 2))
            down(G - 2, 0)
            mix_out(G - 1, range(2, Q))
            down(G - 2, 1)
            ranks(G - 2)
            down(G - 2, 2)
            normed_out(G - 1, 0)
            normed_out(G - 1, 1)
            down(G - 2, 3, end=SM // 2)
            normed_out(G - 1, 2)
            normed_out(G - 1, 3)
            down(G - 2, 3, first=SM // 2)
            logits(G - 1)

            def weights_of(t):
                return pe.value_load(tile_w[0:1, bass.ds(t, 1)], min_val=0, max_val=(E - 1) * 2 * EX_W)

            def need_of(t):
                return pe.value_load(tile_need[0:1, t:t + 1], min_val=EX_PARTS, max_val=E * EX_PARTS)

            pe.wait_ge(prod_done, LB * H)
            pairs_of_banks = ((GATE, UP), (bank[0], bank[1]))
            gate_up(G - 1, 0)
            gate_up(G - 1, 1, pairs_of_banks[1], 1)
            ranks(G - 1)
            with pe.Fori(0, (SM - 2) // 2) as j:
                for u in range(2):
                    gate_up(G - 1, 2 + 2 * j + u, pairs_of_banks[u], 1)
            def tile_in(t, slot, n):
                pe.wait_ge(rows_in[slot], 16 * n)
                transpose_tile(bank[2], lambda lb: xg[slot][:, lb * P:(lb + 1) * P], r_xT)

            down(G - 1, 0)
            down(G - 1, 1)
            pe.wait_ge(tiles_ready, 1)
            down(G - 1, 2)
            first_weights, first_need = weights_of(0), need_of(0)
            tile_in(0, 0, 1)

            def tile_gate_up(t, par, w):
                pe.wait_ge(r_xl, t + 1)
                for half in range(2):
                    last = split_products(
                        bank[half][:, 0:FF],
                        lambda lb: (xgh[par][:, lb * P:(lb + 1) * P], xgl[par][:, lb * P:(lb + 1) * P]),
                        lambda lb: (experts[:, bass.ds(w + (half * LB + lb) * FF, FF)],
                                    experts[:, bass.ds(w + EX_W + (half * LB + lb) * FF, FF)]), LB)
                last.then_inc(r_gu, 1)

            def tile_hidden(t):
                pe.wait_ge(r_hm, t + 1)
                for k in range(FK):
                    c = min(k * P, FF - P)
                    last = nc.tensor.transpose(bank[3][:, k * P:(k + 1) * P], hm[:, c:c + P], ident)
                last.then_inc(r_hT, 1)

            def tile_down(t, w):
                pe.wait_ge(r_hl, t + 1)
                if not isinstance(t, int) or t > 0:
                    pe.wait_ge(r_y, t)
                last = split_products(
                    bank[4],
                    lambda k: (hgh[:, k * P:(k + 1) * P], hgl[:, k * P:(k + 1) * P]),
                    lambda k: (experts[:, bass.ds(w + 2 * LB * FF + k * L, L)],
                               experts[:, bass.ds(w + EX_W + 2 * LB * FF + k * L, L)]), FK)
                last.then_inc(r_down, 1)

            pe.wait_ge(piece_l, first_need)
            down(G - 1, 3, end=SM // 2)
            tile_gate_up(0, 0, first_weights)
            tile_in(1, 1, 1)
            down(G - 1, 3, first=SM // 2)
            following = weights_of(1), need_of(1)
            tile_hidden(0)
            for t in range(1, RING + 1):
                w, need = following
                pe.wait_ge(piece_l, need)
                tile_gate_up(t, t % 2, w)
                tile_in(t + 1, (t + 1) % RING, (t + 1) // RING + 1)
                if t == 1:
                    pe.wait_ge(base_ready, Q * (G - 1) + 1)
                tile_down(t - 1, weights_of(t - 1))
                if t < RING:
                    following = weights_of(t + 1), need_of(t + 1)
                tile_hidden(t)
            pe.wait_ge(piece_l, E * EX_PARTS)
            with pe.Fori(1, (TILES - 3) // RING) as j:
                for u in range(1, RING + 1):
                    t = RING * j + u
                    tile_gate_up(t, u % 2, weights_of(t))
                    tile_in(t + 1, (u + 1) % RING, j + (u + 1) // RING + 1)
                    tile_down(t - 1, weights_of(t - 1))
                    tile_hidden(t)
            for t in range(TILES - 2, TILES):
                tile_gate_up(t, t % 2, weights_of(t))
                if t + 1 < TILES:
                    tile_in(t + 1, (t + 1) % RING, (t + 1) // RING + 1)
                tile_down(t - 1, weights_of(t - 1))
                tile_hidden(t)
            tile_down(TILES - 1, weights_of(TILES - 1))

        @block.scalar
        def _(act):
            def high_parts(s, par, n, reuse=True):
                act.wait_ge(filt_in[par], 16 * n)
                if reuse:
                    act.wait_ge(conv_ready, LB * s - LB)
                nc.scalar.activation(fh[par], backwards(filt_raw[par]), ACT.Copy).then_inc(fh_ready, 1)
                act.wait_ge(kv_ready, s + 1)
                nc.scalar.activation(kvh[par], kv[par], ACT.Copy).then_inc(kvh_ready, 1)

            def layer_norm(src, done):
                for q in range(Q):
                    nc.scalar.activation(normed[:, q, :], src[:, q, :], ACT.Identity, bias=shift[:, q:q + 1],
                                         scale=rstd[:, q:q + 1]).then_inc(done, 1)

            def values(g):
                act.wait_ge(v_shift_ready, g + 1)
                if g == 1:
                    act.wait_ge(skip_ready, Q)
                if g >= 2:
                    act.wait_ge(rows_kept, 16 * (g - 1))
                    act.wait_ge(xfT_ready, Q * (g - 1))
                layer_norm(x_tok[g % 3], v_ready)

            def turned(g):
                if g >= 2:
                    act.wait_ge(mix_done, HG * (g - 1))
                for q in range(Q):
                    act.wait_ge(tokT_ready, Q * g + q + 1)
                    nc.scalar.copy(vT[g % 2].rearrange("p (a t) -> p a t", a=LB)[:, :, q * P:(q + 1) * P],
                                   turn_bank("prep", g, q).rearrange("p (a t) -> p a t", a=LB)
                                   ).then_inc(tokT_done, 1)

            def feed_norm(g):
                act.wait_ge(shift_ready, g + 1)
                layer_norm(x_tok[g % 3], xf_ready)

            def normed_high(g, tiles=range(Q)):
                if g > 0:
                    act.wait_ge(gu_ready, SM * g)
                for q in tiles:
                    act.wait_ge(xfT_ready, Q * g + q + 1)
                    nc.scalar.copy(xfh[:, :, q * P:(q + 1) * P],
                                   turn_bank("xf", g, q).rearrange("p (a t) -> p a t", a=LB)).then_inc(xfh_ready, 1)

            def scores(g):
                act.wait_ge(logit_ready, g + 1)
                nc.scalar.activation(score[:], turn_bank("xf", g, Q)[:, 0:Q * E].rearrange("p (q e) -> p q e", e=E),
                                     ACT.Sigmoid, scale=1 / WS).then_inc(score_ready, 1)

            def gated(g, m, gate=GATE):
                act.wait_ge(gu_ready, SM * g + m + 1)
                p = slice(0, HALF if half_tile(m) else P)
                nc.scalar.activation(silu[p, :], gate[p, :], ACT.Silu, scale=1 / WS).then_inc(silu_ready, 1)
                act.wait_ge(hm_done, SM * g + m + 2)
                if g > 0:
                    act.wait_ge(down_ready, Q * g)
                nc.scalar.copy(hTh[p, bass.ds(m, 1), :].rearrange("p o t -> p (o t)"), hm[p, :]).then_inc(hh_ready, 1)

            def expert(e, *parts):
                for c in parts or range(EX_PARTS):
                    high = experts[:, e * (2 * EX_W) + c * EX_PIECE:e * (2 * EX_W) + (c + 1) * EX_PIECE]
                    if 2 <= e <= 3 and c == 0:
                        act.wait_ge(piece_l, EX_PARTS * e)
                    if e == 4 and c == 0:
                        act.wait_ge(rows_sent, 16 * 2 * Q * (G - 1))
                    if 1 <= e <= 2:
                        act.wait_ge(early_in[e - 1][c], 16)
                    else:
                        shared = len(range(c, SH_PIECES, 2)) if c < 2 else 0
                        act.wait_ge(stage_in[c], 16 * (shared + max(e - 1, 1)))
                    nc.scalar.activation(high, raw_piece(e, c), ACT.Copy, scale=WS).then_inc(piece_h, 1)

            def shared(i, par, n):
                act.wait_ge(stage_in[par], 16 * n)
                raw = stage[par][:, 0:shared_width(i)]
                nc.scalar.activation(shared_piece(i, d_h, gu_h), raw, ACT.Copy, scale=WS)
                nc.scalar.activation(raw, raw, ACT.Copy, scale=WS).then_inc(piece_h, 1)

            act.wait_ge(filt_all_in, 16)
            nc.scalar.activation(filt_all, filt_all, ACT.Copy, scale=WS).then_inc(filt_scaled, 1)
            act.wait_ge(small_in, 32)
            nc.scalar.activation(gate_h[:], gate_raw[:], ACT.Copy, scale=WS).then_inc(gate_split_h, 1)
            values(0)
            turned(0)
            high_parts(0, 0, 1, reuse=False)
            for g in range(G):
                s0 = g * HG
                high_parts(s0 + 1, 1, s0 // 2 + 1, reuse=(g > 0))
                if g == 0:
                    shared(0, 0, 1)
                    shared(1, 1, 1)
                high_parts(s0 + 2, 0, s0 // 2 + 2)
                if g == 0:
                    values(1)
                else:
                    feed_norm(g - 1)
                    normed_high(g - 1, range(0, 2))
                high_parts(s0 + 3, 1, s0 // 2 + 2)
                if g == 0:
                    shared(2, 0, 2)
                    turned(1)
                else:
                    normed_high(g - 1, range(2, Q))
                    scores(g - 1)
                    gated(g - 1, 0)
                with act.Fori(0, 2) as j:
                    for u in range(2):
                        if g == 0:
                            shared(3 + 2 * j + u, (1 + u) % 2, j + 2 + u)
                        high_parts(s0 + 4 + 2 * j + u, u, s0 // 2 + 3 + j)
                        if g > 0:
                            gated(g - 1, 1 + 2 * j + u)
                if g == G - 1:
                    act.wait_ge(mix_done, H)
                    expert(0, 0)
                if g > 0:
                    gated(g - 1, SM - 1)
                if g < G - 1:
                    if g > 0:
                        values(g + 1)
                        turned(g + 1)
                    high_parts(s0 + HG, 0, s0 // 2 + HG // 2 + 1)
                if g == 0:
                    shared(7, 1, 4)
                    shared(8, 0, 5)
            expert(0, 1, 2)
            feed_norm(G - 1)
            normed_high(G - 1)
            expert(0, 3)
            expert(1, 0, 1)
            scores(G - 1)
            expert(1, 2, 3)
            gates = (GATE, bank[0])
            for m in range(SM):
                gated(G - 1, m, gates[m % 2])
                for e, c in pieces_after[m]:
                    expert(e, c)

            def tile_high(t, par):
                act.wait_ge(r_xT, t + 1)
                nc.scalar.copy(xgh[par], bank[2]).then_inc(r_xh, 1)

            act.wait_ge(base_stored, 32 * (G - 1))
            expert(E - 3)
            tile_high(0, 0)
            expert(E - 2)

            def tile_silu(t):
                act.wait_ge(r_gu, t + 1)
                nc.scalar.activation(silu[:, 0:FF], bank[0][:, 0:FF], ACT.Silu, scale=1 / WS).then_inc(r_silu, 1)

            def tile_out(t, slot, n):
                act.wait_ge(ids_in[slot], 16 * n)
                act.wait_ge(r_down, t + 1)
                if not isinstance(t, int) or t >= RING:
                    act.wait_ge(added, 16 * (t - RING + 1))
                nc.scalar.activation(yg[slot], bank[4], ACT.Copy, scale=ids[slot][:, 1:2].bitcast(F32)
                                     ).then_inc(r_y, 1)

            def tile_hidden_high(t):
                act.wait_ge(r_hT, t + 1)
                nc.scalar.copy(hgh, bank[3][:, 0:FK * P]).then_inc(r_hh, 1)

            tile_silu(0)
            tile_high(1, 1)
            tile_hidden_high(0)
            act.wait_ge(down_ready, Q * G)
            for t in range(1, RING + 1):
                tile_silu(t)
                tile_high(t + 1, (t + 1) % 2)
                if t == 1:
                    act.wait_ge(base_stored, 32 * G)
                tile_out(t - 1, (t - 1) % RING, (t - 1) // RING + 1)
                tile_hidden_high(t)
                if t <= 2:
                    expert(E - 1, *(first_half, second_half)[t - 1])
            with act.Fori(1, (TILES - 3) // RING) as j:
                for u in range(1, RING + 1):
                    t = RING * j + u
                    tile_silu(t)
                    tile_high(t + 1, (u + 1) % 2)
                    tile_out(t - 1, u - 1, j + 1)
                    tile_hidden_high(t)
            for t in range(TILES - 2, TILES):
                tile_silu(t)
                if t + 1 < TILES:
                    tile_high(t + 1, (t + 1) % 2)
                tile_out(t - 1, (t - 1) % RING, (t - 1) // RING + 1)
                tile_hidden_high(t)
            tile_out(TILES - 1, (TILES - 1) % RING, (TILES - 1) // RING + 1)

        @block.vector
        def _(dve):
            steps = [0]

            def link(*ins):
                for i in ins:
                    i.then_inc(dve_step, 1)
                    steps[0] += 1
                dve.wait_ge(dve_step, steps[0])

            def low_parts(s, par):
                dve.wait_ge(kvh_ready, s + 1)
                nc.vector.tensor_tensor(kvl[par], kv[par], kvh[par], ALU.subtract).then_inc(kvl_ready, 1)

            def finish(s, h, g):
                products(s, h, g)
                total(s, h)

            def products(s, h, g):
                if not isinstance(s, int) or s > 0:
                    dve.wait_ge(mix_done, s)
                for n in range(LB):
                    dve.wait_ge(conv_ready, LB * s + n + 1)
                    c = heads(cT[g % 2])[:, n * B:(n + 1) * B, bass.ds(h * NH, NH)]
                    nc.vector.tensor_tensor(
                        prod[:, n * COLS:(n + 1) * COLS].rearrange("p (b i j) -> p b i j", i=NH, j=NH),
                        bank[n].rearrange("p (b i j) -> p b i j", i=NH, j=NH),
                        c[:, :, :, None].to_broadcast([P, B, NH, NH]), ALU.mult).then_inc(prod_done, 1)

            def total(s, h):
                dve.wait_ge(prod_done, LB * s + LB)
                nc.vector.tensor_reduce(heads(mixT)[:, :, bass.ds(h * NH, NH)],
                                        prod.rearrange("p (a i j) -> p a j i", i=NH, j=NH), AX_X, ALU.add
                                        ).then_inc(mix_done, 1)

            def moments(src):
                link(*[nc.vector.bn_stats(stats[:, q, :], src[:, q, :]) for q in range(Q)])
                link(*[nc.vector.bn_aggr(meanvar[:, q, :], stats[:, q, :]) for q in range(Q)])
                nc.vector.tensor_scalar(var_eps[:], meanvar[:, :, 1], EPS, None, ALU.add).then_inc(var_ready, 1)

            def shift_by(done):
                nc.vector.scalar_tensor_tensor(out=shift[:], in0=meanvar[:, :, 0], scalar=-1.0, in1=rstd[:],
                                               op0=ALU.mult, op1=ALU.mult).then_inc(done, 1)

            def value_moments(g):
                dve.wait_ge(x_in[g], 32)
                moments(x_tok[g % 3])

            def values(g):
                dve.wait_ge(rstd_ready, (0 if g == 0 else 2 * g - 1) + 1)
                shift_by(v_shift_ready)

            def skip_product(g, q):
                if q >= 2:
                    dve.wait_ge(skipsum_ready, Q * g + q - 1)
                dve.wait_ge(v_ready, Q * g + q + 1)
                dve.wait_ge(ctx_in[g], 32)
                nc.vector.scalar_tensor_tensor(out=skipped[q % 2][:], in0=ctx_tok[:, q, :], scalar=skip_col[:, g:g + 1],
                                               in1=normed[:, q, :], op0=ALU.mult, op1=ALU.mult).then_inc(skip_ready, 1)

            def skip_term(g, q):
                dve.wait_ge(skipsum_ready, Q * g + q + 1)
                if q + 2 < Q:
                    skip_product(g, q + 2)
                c, r = ctx_tok[:, q, :], x_tok[g % 3][:, q, :]
                t = nc.vector.tensor_tensor(c, turn_bank("prep", g, 2 * Q + q), c, ALU.mult)
                link(t)
                nc.vector.tensor_tensor(r, r, c, ALU.add).then_inc(skip_done, 1)

            def normed_low(g, tiles=range(Q)):
                for q in tiles:
                    dve.wait_ge(xfh_ready, Q * g + q + 1)
                    c = slice(q * P, (q + 1) * P)
                    nc.vector.tensor_tensor(xfl[:, :, c], turn_bank("xf", g, q).rearrange("p (a t) -> p a t", a=LB),
                                            xfh[:, :, c], ALU.subtract).then_inc(xfl_ready, 1)

            def pick(g):
                dve.wait_ge(score_ready, g + 1)
                link(*[nc.vector.max(top[:, q, :], score[:, q, :]) for q in range(Q)])
                link(*[nc.vector.max_index(topi[:, q, :], top[:, q, :], score[:, q, :]) for q in range(Q)])
                link(nc.vector.tensor_copy(topf[:], topi[:, :, 0:2]))
                shape = [P, Q, 2, E]
                for k in range(2):
                    shape = [P, Q, E]
                    i = nc.vector.tensor_tensor(onehot[:, :, k, :], iota8[:, None, :].to_broadcast(shape),
                                                topf[:, :, k:k + 1].to_broadcast(shape), ALU.is_equal)
                    link(i)
                nc.vector.tensor_tensor(picked[:, 0:Q, :], onehot[:, :, 0, :], onehot[:, :, 1, :], ALU.add
                                        ).then_inc(picked_ready, 1)

            def pairs(g):
                t = turn_bank("rank", g, 0)
                if g > 0:
                    dve.wait_ge(pairs_stored, 16 * 2 * Q * g)
                    dve.wait_ge(rows_sent, 16 * 2 * Q * g)
                dve.wait_ge(rank_ready, g + 1)
                link(nc.vector.tensor_tensor(rank[:], t[:, 0:Q * E].rearrange("p (q e) -> p q e", e=E),
                                             next_row[:, None, :].to_broadcast([P, Q, E]), ALU.add))
                nc.vector.tensor_tensor(next_row[:], next_row[:], t[:, Q * E:(Q + 1) * E], ALU.add
                                        ).then_inc(rank_used, 1)
                for k in range(2):
                    i = nc.vector.tensor_tensor(rankhot[:, :, k, :], onehot[:, :, k, :], rank[:], ALU.mult)
                    link(i)
                link(nc.vector.tensor_reduce(rowf[:], rankhot[:], AX_X, ALU.add))
                link(nc.vector.tensor_copy(row[:], rowf[:]),
                     nc.vector.tensor_scalar(pad_row[:], next_row[:], part_no, None, ALU.add),
                     nc.vector.tensor_scalar(tok_ids[:], row_base, float(RG * g), None, ALU.add),
                     nc.vector.tensor_tensor(wsum[:], top[:, :, 0], top[:, :, 1], ALU.add))
                link(nc.vector.tensor_scalar(wsum[:], wsum[:], 1e-20, None, ALU.add))
                link(nc.vector.reciprocal(winv[:], wsum[:]))
                link(nc.vector.tensor_tensor(wtop[:], top[:, :, 0:2], winv[:, :, None].to_broadcast([P, Q, 2]), ALU.mult))
                link(nc.vector.tensor_scalar(pair[:, :, :, 1].bitcast(F32), wtop[:], ROUTE_SCALE / WS, None, ALU.mult),
                     nc.vector.tensor_copy(pair[:, :, 0, 0], tok_ids[:]))
                nc.vector.tensor_copy(pair[:, :, 1, 0], tok_ids[:]).then_inc(pair_ready, 1)

            def tile_table():
                dve.wait_ge(rank_used, G)
                link(nc.vector.tensor_tensor(n_f[:], next_row[0:1, :], first_row[0:1, :], ALU.subtract))
                link(nc.vector.tensor_scalar(n_i[:], n_f[:], float(P - 1), None, ALU.add))
                link(nc.vector.tensor_scalar(n_i[:], n_i[:], P.bit_length() - 1, None, ALU.arith_shift_right))
                link(nc.vector.tensor_copy(n_f[:], n_i[:]))
                link(nc.vector.tensor_tensor_scan(n_end[:], ones[0:1, 0:E], n_f[:], 0.0, ALU.mult, ALU.add))
                shape = [1, SLOTS, E]
                link(nc.vector.tensor_tensor(past[:], tile_no[:, :, None].to_broadcast(shape),
                                             n_end[:, None, :].to_broadcast(shape), ALU.is_ge))
                link(nc.vector.tensor_tensor(past_n[:], past[:], n_f[:, None, :].to_broadcast(shape), ALU.mult),
                     nc.vector.tensor_reduce(t_exp[:], past[:], AX_X, ALU.add))
                link(nc.vector.tensor_reduce(t_start, past_n[:], AX_X, ALU.add),
                     nc.vector.scalar_tensor_tensor(out=t_row[:], in0=t_exp[:], scalar=float(EROWS // P), in1=tile_no,
                                                    op0=ALU.mult, op1=ALU.add))
                link(nc.vector.tensor_tensor(t_row[:], t_row[:], t_start, ALU.subtract),
                     nc.vector.tensor_scalar(tile_w[:], t_exp[:], float(E - 1), float(2 * EX_W), ALU.min, ALU.mult))
                link(nc.vector.tensor_scalar(t_exp[:], t_exp[:], float(E - 1), None, ALU.min))
                link(nc.vector.tensor_scalar(tile_need[:], t_exp[:], float(EX_PARTS), float(EX_PARTS), ALU.mult, ALU.add))
                nc.vector.tensor_scalar(tile_row[:], t_row[:], float(E * EROWS // P), float(P), ALU.min, ALU.mult
                                        ).then_inc(tiles_ready, 1)

            def gated(g, m, up=UP):
                dve.wait_ge(silu_ready, SM * g + m + 1)
                if not isinstance(m, int) or SM * g + m > 0:
                    dve.wait_ge(hl_ready, SM * g + m)
                p = slice(0, HALF if half_tile(m) else P)
                if half_tile(m):
                    up = GATE[HALF:2 * HALF, :]
                nc.vector.scalar_tensor_tensor(out=hm[p, :], in0=up, scalar=1 / WS, in1=silu[p, :], op0=ALU.mult,
                                               op1=ALU.mult).then_inc(hm_done, 1)
                dve.wait_ge(hh_ready, SM * g + m + 1)
                one = "p o t -> p (o t)"
                nc.vector.tensor_tensor(hTl[p, bass.ds(m, 1), :].rearrange(one), hm[p, :],
                                        hTh[p, bass.ds(m, 1), :].rearrange(one), ALU.subtract).then_inc(hl_ready, 1)

            def add_shared(g, q):
                dve.wait_ge(down_ready, Q * g + q + 1)
                r = x_tok[g % 3][:, q, :]
                nc.vector.scalar_tensor_tensor(out=r, in0=down_bank(g, q), scalar=1 / WS, in1=r, op0=ALU.mult,
                                               op1=ALU.add).then_inc(base_ready, 1)

            def mixed(g):
                for q in range(Q):
                    if g == G - 1 and q == 2:
                        expert(0, 1)
                    dve.wait_ge(outT_ready, Q * g + q + 1)
                    r = x_tok[g % 3][:, q, :]
                    nc.vector.scalar_tensor_tensor(out=r, in0=turn_bank("out", g, q), scalar=1 / WS, in1=r,
                                                   op0=ALU.mult, op1=ALU.add).then_inc(x1_done, 1)
                dve.wait_ge(x1_done, Q * (g + 1))
                moments(x_tok[g % 3])

            def mixed_shift(g):
                dve.wait_ge(rstd_ready, (2 * g + 2 if g < G - 1 else 2 * G - 1) + 1)
                shift_by(shift_ready)

            def expert_piece(e, c):
                at = e * (2 * EX_W) + c * EX_PIECE
                dve.wait_ge(piece_h, SH_PIECES + e * EX_PARTS + c + 1)
                nc.vector.scalar_tensor_tensor(
                    out=experts[:, bass.ds(at + EX_W, EX_PIECE)], in0=raw_piece(e, c), scalar=WS,
                    in1=experts[:, bass.ds(at, EX_PIECE)], op0=ALU.mult, op1=ALU.subtract).then_inc(piece_l, 1)

            def expert(e, *parts):
                for c in parts or range(EX_PARTS):
                    expert_piece(e, c)

            value_moments(0)
            values(0)
            dve.wait_ge(const_in, 16)
            nc.vector.tensor_copy(next_row[:], first_row).then_inc(hm_done, 1)
            nc.vector.tensor_copy(masks16[:], con[:, 2 * P:4 * P])
            nc.vector.tensor_scalar(picked[:, Q, :], iota8, 0.0, None, ALU.mult)
            dve.wait_ge(gate_split_h, 1)
            nc.vector.scalar_tensor_tensor(out=gate_l[:], in0=gate_raw[:], scalar=WS, in1=gate_h[:], op0=ALU.mult,
                                           op1=ALU.subtract).then_inc(gate_split_l, 1)
            skip_product(0, 0)
            skip_product(0, 1)
            value_moments(1)
            skip_term(0, 0)
            skip_term(0, 1)
            low_parts(0, 0)
            skip_term(0, 2)
            skip_term(0, 3)
            for g in range(G):
                s0 = g * HG
                low_parts(s0 + 1, 1)
                products(s0, 0, g)
                if g == 0:
                    total(s0, 0)
                    values(1)
                else:
                    mixed(g - 1)
                    total(s0, 0)
                    mixed_shift(g - 1)
                low_parts(s0 + 2, 0)
                products(s0 + 1, 1, g)
                if g > 0:
                    normed_low(g - 1, range(0, 2))
                total(s0 + 1, 1)
                if g > 0:
                    normed_low(g - 1, range(2, Q))
                low_parts(s0 + 3, 1)
                if g == 0:
                    skip_product(1, 0)
                    skip_product(1, 1)
                finish(s0 + 2, 2, g)
                if g == 0:
                    skip_term(1, 0)
                    skip_term(1, 1)
                else:
                    pick(g - 1)
                    gated(g - 1, 0)
                with dve.Fori(0, 2) as j:
                    for u in range(2):
                        h = 4 + 2 * j + u
                        low_parts(s0 + h, u)
                        finish(s0 + h - 1, h - 1, g)
                        if g > 0:
                            gated(g - 1, 1 + 2 * j + u)
                if g == 0:
                    low_parts(s0 + HG, 0)
                finish(s0 + HG - 1, HG - 1, g)
                if g == 0:
                    skip_term(1, 2)
                    skip_term(1, 3)
                else:
                    if g == G - 1:
                        expert(0, 0)
                    gated(g - 1, SM - 1)
                    if g < G - 1:
                        pairs(g - 1)
                        value_moments(g + 1)
                        values(g + 1)
                if 0 < g < G - 1:
                    add_shared(g - 1, 0)
                    add_shared(g - 1, 1)
                    skip_product(g + 1, 0)
                    skip_product(g + 1, 1)
                    skip_term(g + 1, 0)
                    add_shared(g - 1, 2)
                    skip_term(g + 1, 1)
                    skip_term(g + 1, 2)
                    low_parts(s0 + HG, 0)
                    add_shared(g - 1, 3)
                    skip_term(g + 1, 3)
            mixed(G - 1)
            add_shared(G - 2, 0)
            mixed_shift(G - 1)
            add_shared(G - 2, 1)
            pairs(G - 2)
            add_shared(G - 2, 2)
            expert(0, 2)
            normed_low(G - 1, range(0, 2))
            normed_low(G - 1, range(2, Q))
            add_shared(G - 2, 3)
            expert(0, 3)
            expert(1, 0)
            pick(G - 1)
            expert(1, 1, 2, 3)
            ups = (UP, bank[1])
            for m in range(SM):
                gated(G - 1, m, ups[m % 2])
                for e, c in pieces_after[m]:
                    expert(e, c)
                    if m == c == 0:
                        pairs(G - 1)
                if m == 3:
                    tile_table()

            def tile_low(t, par):
                dve.wait_ge(r_xh, t + 1)
                nc.vector.tensor_tensor(xgl[par], bank[2], xgh[par], ALU.subtract).then_inc(r_xl, 1)

            expert(E - 3)
            tile_low(0, 0)
            add_shared(G - 1, 0)
            add_shared(G - 1, 1)
            expert(E - 2)

            def tile_gated(t):
                dve.wait_ge(r_silu, t + 1)
                nc.vector.scalar_tensor_tensor(out=hm[:, 0:FF], in0=bank[1][:, 0:FF], scalar=1 / WS,
                                               in1=silu[:, 0:FF], op0=ALU.mult, op1=ALU.mult).then_inc(r_hm, 1)

            def tile_hidden_low(t):
                dve.wait_ge(r_hh, t + 1)
                nc.vector.tensor_tensor(hgl, bank[3][:, 0:FK * P], hgh, ALU.subtract).then_inc(r_hl, 1)

            tile_gated(0)
            tile_low(1, 1)
            tile_hidden_low(0)
            add_shared(G - 1, 2)
            add_shared(G - 1, 3)
            for t in range(1, 3):
                tile_gated(t)
                tile_low(t + 1, (t + 1) % 2)
                tile_hidden_low(t)
                expert(E - 1, *(first_half, second_half)[t - 1])
            with dve.Fori(1, (TILES - 3) // 2) as j:
                for u in range(1, 3):
                    t = 2 * j + u
                    tile_gated(t)
                    tile_low(t + 1, (u + 1) % 2)
                    tile_hidden_low(t)
            for t in range(TILES - 2, TILES):
                tile_gated(t)
                if t + 1 < TILES:
                    tile_low(t + 1, (t + 1) % 2)
                tile_hidden_low(t)


def constants():
    import numpy as np

    con = np.zeros((P, CONST_W), np.float32)
    p = np.arange(P)
    con[:, 0:P] = np.eye(P)
    con[:, P:2 * P] = p[:, None] // NH == p[None, :] // NH
    con[:, 2 * P:3 * P] = p[:, None] < p[None, :]
    con[:, 3 * P:4 * P] = 1
    c = 4 * P
    con[:, c:c + 8] = np.arange(8)
    con[:, c + 8:c + 12] = -0.5
    con[:, c + 12:c + 20] = np.arange(E) * EROWS
    con[:, c + 20:c + 20 + SLOTS] = np.arange(SLOTS)
    con[:, -1] = p
    con[:, c + 20 + SLOTS:-1] = (np.arange(Q)[None] * 2 + p[:, None] // RG) * S + p[:, None] % RG
    table = np.zeros((TROWS, 2), np.int32)
    table[:, 0] = T + np.arange(TROWS) % P
    return con, table, np.zeros((P, L), np.float32)


def kernel(x, fside_S2_0, ctx_2048, L0_xattn_k, L0_ffn_gate_w, L0_ffn_shared_wg, L0_ffn_shared_wu, L0_ffn_shared_wd,
           L0_ffn_exp_wg, L0_ffn_exp_wu, L0_ffn_exp_wd):
    import numpy as np
    import concourse.bacc as bacc
    from concourse.bass_utils import run_bass_kernel_spmd

    def rows(w, n):
        w = w.reshape(*w.shape[:-2], n, P, w.shape[-1])
        w = np.moveaxis(w, -3, -2)
        return w.reshape(*w.shape[:-2], n * w.shape[-1])

    def padded(w, n):
        return np.concatenate([w, np.zeros((*w.shape[:-1], n - w.shape[-1]), w.dtype)], -1)

    a = {k: np.asarray(v) for k, v in dict(
        x=x, skip=fside_S2_0, ctx=ctx_2048, k=L0_xattn_k, gate=L0_ffn_gate_w, sg=L0_ffn_shared_wg, su=L0_ffn_shared_wu,
        sd=L0_ffn_shared_wd, eg=L0_ffn_exp_wg, eu=L0_ffn_exp_wu, ed=L0_ffn_exp_wd).items()}
    con, table, zeros = constants()
    gate, up, whole = a["sg"].T, a["su"].T, SFF - HALF
    gu = np.concatenate([gate[:, whole:], up[:, whole:], gate[:, 0:whole], up[:, 0:whole]], -1)
    sd = np.concatenate([padded(a["sd"][:, whole:], P), a["sd"][:, 0:whole]], -1).T
    ed = a["ed"]
    whole = (FK - 1) * P
    last = np.concatenate([np.zeros((E, L, FK * P - FF), ed.dtype), ed[:, :, whole:]], -1)
    ed = np.concatenate([ed[:, :, 0:whole], last], -1)
    t = lambda w: np.swapaxes(w, -1, -2)
    arrays = {
        "x": a["x"], "ctx": a["ctx"],
        "ctx_hidden": a["ctx"].reshape(B, G, RG, LB, P).transpose(1, 4, 3, 0, 2).reshape(G, P, LB * TG),
        "skip": np.tile(a["skip"].reshape(G, RG).T, (2, 1)),
        "krev": padded(a["k"][:, ::-1], KREV),
        "gate_w": rows(a["gate"].T, LB),
        "shared_w": padded(np.concatenate([rows(sd, SM), rows(gu, LB)], -1), SH_PIECES * SH_PIECE),
        "expert_w": np.concatenate([rows(t(a["eg"]), LB), rows(t(a["eu"]), LB), rows(t(ed), FK)], -1),
        "consts": con, "table0": table, "zeros": zeros,
    }
    arrays = {f"in_{k}": np.ascontiguousarray(v) for k, v in arrays.items()}
    nc = bacc.Bacc("TRN2", target_bir_lowering=False, num_devices=1)
    args = [nc.dram_tensor(k, v.shape, mybir.dt.from_np(v.dtype), kind="ExternalInput").ap() for k, v in arrays.items()]
    out = nc.dram_tensor("out", (T + P, L), F32, kind="ExternalOutput").ap()
    xattn_moe(nc, *args, out)
    r = run_bass_kernel_spmd(nc, [arrays], core_ids=[0])
    return r.results[0]["out"][0:T].reshape(B, S, L)
```
